# Optimizing a Trainium2 kernel written in Bass

```python
import numpy as np
import jax
import jax.numpy as jnp

def _softmax(x, axis=-1):
    return jax.nn.softmax(x, axis=axis)

def _gelu(x):
    return jax.nn.gelu(x, approximate=True)

def _silu(x):
    return jax.nn.silu(x)

def _sigmoid(x):
    return jax.nn.sigmoid(x)

def _layernorm(x, axis=-1, eps=1e-05):
    m = jnp.mean(x, axis=axis, keepdims=True)
    v = jnp.var(x, axis=axis, keepdims=True)
    return (x - m) / jnp.sqrt(v + eps)

def _scatter_add(tgt, idx, src, axis=0):
    return tgt.at[idx].add(src)

def _segment_sum(src, seg, n):
    return jax.ops.segment_sum(src, seg, n)
kernel_name = 'mk_prb_d1_jaxref_r8_953e90'

def setup_inputs(seed: int=0):
    np.random.seed(seed)
    _w = jnp.asarray

    def _L0_attn_setup():
        import math
        import jax, jax.numpy as jnp
        import numpy as np
        B, S, D, H = (4, 128, 128, 16)
        HD = D // H
        EPS = 1e-05

        def _sinusoidal_encodings(length, d):
            pos = jnp.arange(length, dtype=jnp.float32)
            inv_freq = 1.0 / 10000.0 ** (jnp.arange(0.0, d, 2.0) / d)
            angles = pos[:, None] * inv_freq[None, :]
            enc = jnp.zeros((length, d), dtype=jnp.float32)
            enc = enc.at[:, 0::2].set(jnp.sin(angles))
            enc = enc.at[:, 1::2].set(jnp.cos(angles))
            return enc

        def _relative_shift(emb):
            b, h, l1, l2 = emb.shape
            padded = jnp.concatenate([jnp.zeros((b, h, l1, 1), emb.dtype), emb], axis=-1)
            padded = padded.reshape(b, h, l2 + 1, l1)
            return padded[:, :, 1:, :].reshape(b, h, l1, l2)
        key = jax.random.key(seed)
        ks = jax.random.split(key, 12)
        s = 0.02
        inp = {'x': jax.random.normal(ks[0], (B, S, D), dtype=jnp.float32), 'Wq': jax.random.normal(ks[1], (D, D), dtype=jnp.float32) * s, 'bq': jnp.zeros((D,), jnp.float32), 'Wk': jax.random.normal(ks[2], (D, D), dtype=jnp.float32) * s, 'bk': jnp.zeros((D,), jnp.float32), 'Wv': jax.random.normal(ks[3], (D, D), dtype=jnp.float32) * s, 'bv': jnp.zeros((D,), jnp.float32), 'Wpos': jax.random.normal(ks[4], (D, D), dtype=jnp.float32) * s, 'Wf': jax.random.normal(ks[5], (D, D), dtype=jnp.float32) * s, 'bf': jnp.zeros((D,), jnp.float32), 'u': jax.random.normal(ks[6], (H, HD), dtype=jnp.float32) * s, 'v': jax.random.normal(ks[7], (H, HD), dtype=jnp.float32) * s, 'gamma': jnp.ones((D,), jnp.float32), 'beta': jnp.zeros((D,), jnp.float32)}
        return inp
    _L0_attn_in = _L0_attn_setup()

    def _L0_ffn_setup():
        import jax, jax.numpy as jnp
        import numpy as np
        B, T, D, F, E, TOPK = (4, 256, 128, 344, 8, 2)
        key = jax.random.key(seed)
        k1, k2, k3, k4 = jax.random.split(key, 4)
        x = jax.random.normal(k1, (B, T, D), dtype=jnp.float32)
        W13 = jax.random.normal(k2, (E, D, 2 * F), dtype=jnp.float32) * 0.02
        W2 = jax.random.normal(k3, (E, F, D), dtype=jnp.float32) * 0.02
        Wr = jax.random.normal(k4, (D, E), dtype=jnp.float32) * 0.02
        return {'x': x, 'W13': W13, 'W2': W2, 'Wr': Wr}
    _L0_ffn_in = _L0_ffn_setup()
    _d = {'L0_attn_x': _L0_attn_in['x'], 'L0_attn_Wq': _L0_attn_in['Wq'], 'L0_attn_bq': _L0_attn_in['bq'], 'L0_attn_Wk': _L0_attn_in['Wk'], 'L0_attn_bk': _L0_attn_in['bk'], 'L0_attn_Wv': _L0_attn_in['Wv'], 'L0_attn_bv': _L0_attn_in['bv'], 'L0_attn_Wpos': _L0_attn_in['Wpos'], 'L0_attn_Wf': _L0_attn_in['Wf'], 'L0_attn_bf': _L0_attn_in['bf'], 'L0_attn_u': _L0_attn_in['u'], 'L0_attn_v': _L0_attn_in['v'], 'L0_attn_gamma': _L0_attn_in['gamma'], 'L0_attn_beta': _L0_attn_in['beta'], 'L0_ffn_W13': _L0_ffn_in['W13'], 'L0_ffn_W2': _L0_ffn_in['W2'], 'L0_ffn_Wr': _L0_ffn_in['Wr']}
    _x0 = _d['L0_attn_x']
    _d['L0_attn_x'] = jax.random.normal(jax.random.fold_in(jax.random.key(seed), 1), (8, 512, 128), dtype=_x0.dtype)
    del _x0
    return _d

def reference(L0_attn_x, L0_attn_Wq, L0_attn_bq, L0_attn_Wk, L0_attn_bk, L0_attn_Wv, L0_attn_bv, L0_attn_Wpos, L0_attn_Wf, L0_attn_bf, L0_attn_u, L0_attn_v, L0_attn_gamma, L0_attn_beta, L0_ffn_W13, L0_ffn_W2, L0_ffn_Wr):

    def _L0_attn_ref(x, Wq, bq, Wk, bk, Wv, bv, Wpos, Wf, bf, u, v, gamma, beta):
        import math
        import jax, jax.numpy as jnp
        import numpy as np
        B, S, D, H = (4, 128, 128, 16)
        HD = D // H
        EPS = 1e-05

        def _sinusoidal_encodings(length, d):
            pos = jnp.arange(length, dtype=jnp.float32)
            inv_freq = 1.0 / 10000.0 ** (jnp.arange(0.0, d, 2.0) / d)
            angles = pos[:, None] * inv_freq[None, :]
            enc = jnp.zeros((length, d), dtype=jnp.float32)
            enc = enc.at[:, 0::2].set(jnp.sin(angles))
            enc = enc.at[:, 1::2].set(jnp.cos(angles))
            return enc

        def _relative_shift(emb):
            b, h, l1, l2 = emb.shape
            padded = jnp.concatenate([jnp.zeros((b, h, l1, 1), emb.dtype), emb], axis=-1)
            padded = padded.reshape(b, h, l2 + 1, l1)
            return padded[:, :, 1:, :].reshape(b, h, l1, l2)
        b, s, d = x.shape
        mu = jnp.mean(x, axis=-1, keepdims=True)
        var = jnp.mean((x - mu) ** 2, axis=-1, keepdims=True)
        xn = (x - mu) * jax.lax.rsqrt(var + EPS) * gamma + beta
        pe = _sinusoidal_encodings(s, d)
        q = (xn @ Wq + bq).reshape(b, s, H, HD)
        k = (xn @ Wk + bk).reshape(b, s, H, HD)
        val = (xn @ Wv + bv).reshape(b, s, H, HD)
        p = (pe @ Wpos).reshape(s, H, HD)
        AC = jnp.einsum('bihd,bjhd->bhij', q + u, k)
        BD = jnp.einsum('bihd,jhd->bhij', q + v, p)
        BD = _relative_shift(BD)
        attn = jax.nn.softmax((AC + BD) / math.sqrt(d), axis=-1)
        out = jnp.einsum('bhij,bjhd->bihd', attn, val).reshape(b, s, d)
        out = out @ Wf + bf
        return out

    def _L0_ffn_ref(x, W13, W2, Wr):
        import jax, jax.numpy as jnp
        import numpy as np
        B, T, D, F, E, TOPK = (4, 256, 128, 344, 8, 2)
        b, t, d = x.shape
        xf = x.reshape(-1, d)
        n = xf.shape[0]
        logits = xf @ Wr
        probs = jax.nn.softmax(logits, axis=-1)
        top_probs, top_idx = jax.lax.top_k(probs, TOPK)
        top_probs = top_probs / top_probs.sum(axis=-1, keepdims=True)
        cw = jnp.zeros((n, E), dtype=xf.dtype).at[jnp.arange(n)[:, None], top_idx].add(top_probs)
        out = jnp.zeros_like(xf)
        for e in range(E):
            x13 = xf @ W13[e]
            x1, x3 = jnp.split(x13, 2, axis=-1)
            h = jax.nn.silu(x1) * x3
            out = out + cw[:, e:e + 1] * (h @ W2[e])
        return out.reshape(b, t, d)
    x = L0_attn_x
    xn = _layernorm(x, axis=-1)
    x = x + _L0_attn_ref(xn, L0_attn_Wq, L0_attn_bq, L0_attn_Wk, L0_attn_bk, L0_attn_Wv, L0_attn_bv, L0_attn_Wpos, L0_attn_Wf, L0_attn_bf, L0_attn_u, L0_attn_v, L0_attn_gamma, L0_attn_beta) + _L0_ffn_ref(xn, L0_ffn_W13, L0_ffn_W2, L0_ffn_Wr)
    return x

_drawn_inputs = setup_inputs


def setup_inputs(seed=0):
    import zlib

    import numpy as np

    out = dict(_drawn_inputs(seed))
    spreads = {'L0_attn_bq': (0.0, 2.0),
     'L0_attn_bk': (0.0, 2.0),
     'L0_attn_bv': (0.0, 2.0),
     'L0_attn_bf': (0.0, 0.421),
     'L0_attn_gamma': (1.0, 0.6),
     'L0_attn_beta': (0.0, 0.8)}
    factors = {'L0_attn_Wq': 8.0,
     'L0_attn_Wk': 8.0,
     'L0_attn_Wv': 8.0,
     'L0_attn_Wpos': 24.894,
     'L0_attn_u': 64.0,
     'L0_attn_v': 64.0,
     'L0_ffn_W13': 8.0,
     'L0_ffn_W2': 8.0,
     'L0_ffn_Wr': 8.0}
    for name, (base, spread) in spreads.items():
        noise = np.random.default_rng([zlib.crc32(name.encode()), seed]).standard_normal(out[name].shape)
        drawn = base * np.exp(spread * noise) if base else spread * noise
        out[name] = jnp.asarray(drawn.astype(out[name].dtype))
    for name, factor in factors.items():
        out[name] = (out[name] * factor).astype(out[name].dtype)
    return out
```

```python
from contextlib import ExitStack

import concourse.bass as bass
from concourse import mybir

ALU = mybir.AluOpType
ACT = mybir.ActivationFunctionType
AX = mybir.AxisListType
F32 = mybir.dt.float32
F16 = mybir.dt.float16
ds = bass.ds

P = 128
EPS = 1e-5
TOPK = 2


def build(nc, x, Wq, bq, Wk, bk, Wv, bv, Wpos, Wf, bf, u, v, gamma, beta, W13, W2, Wr, peT, ident, sel, tri, out):
    B, S, D = x.shape
    H, HD = u.shape
    E, F, _ = W2.shape
    T = S // P
    GH = 4
    NG = H // GH
    N = B * NG
    U = GH * T
    FT = -(-F // P)
    FW = [min(P, F - P * f) for f in range(FT)]
    NU = B * E // N
    SCALE = 1.0 / float(D) ** 0.5
    SLOT = P // GH
    assert D == P and S == T * P and SLOT == 4 * HD and NU == 2 and E == 8 and NG == 4

    HIDDEN_AT = {0: (0, 0), 2: (0, 1), 4: (0, 2), 8: (1, 0), 10: (1, 1), 12: (1, 2)}
    DOWN_AT = {6: [(0, 0), (0, 1)], 7: [(0, 2), (0, 3)], 14: [(1, 0), (1, 1)], 15: [(1, 2), (1, 3)]}

    with ExitStack() as ctx:
        def sb(name, shape, dt=F32):
            return ctx.enter_context(nc.sbuf_tensor(name, shape, dt))

        def sem(name):
            return ctx.enter_context(nc.semaphore(name))

        scratch = nc.dram_tensor("scratch", [GH, S * (S + 1)], F32).ap()

        acc = sb("acc", [P, B, T, D])
        xnT = sb("xnT", [P, 2, B, S], F16)
        quT = sb("quT", [P, 2, B, S], F16)
        qvT = sb("qvT", [P, 2, B, S], F16)
        kT = sb("kT", [P, 2, B, S], F16)
        vall = sb("vall", [P, N, 4, GH * HD])
        w13 = sb("w13", [P, 2, E, 2 * F], F16)
        w2 = sb("w2", [P, 2, E, FT, D], F16)
        pall = sb("pall", [P, NG, S], F16)
        idf = sb("idf", [P, P])
        selb = sb("selb", [P, 2, 2, NG, P], F16)
        cw = sb("cw", [P, B * T, E])
        wf_sb = sb("wf_sb", [P, D])
        sums = sb("sums", [P, N, U])
        rs = sb("rs", [P, U])
        nmax = sb("nmax", [P, U])
        bdr = sb("bdr", [P, 2, T, S])
        bdw = sb("bdw", [P, 2, T, S + 1])
        qus = sb("qus", [P, S], F16)
        qvs = sb("qvs", [P, S], F16)
        ks = sb("ks", [P, S], F16)
        ps = sb("ps", [P, S], F16)
        Sb = sb("Sb", [P, 2, S])
        Pb = sb("Pb", [P, 2, S])
        PTb = sb("PTb", [P, 2, S])
        th = sb("th", [P, S])
        ab = sb("ab", [P, S])
        hb = sb("hb", [P, S])
        hh = sb("hh", [P, FT, S], F16)
        hl = sb("hl", [P, FT, S], F16)

        bank = [ctx.enter_context(nc.psum_tensor(f"bank{i}", [P, 512], F32)) for i in range(8)]
        ac_ps, bd_ps, tp_ps, x1_ps, x3_ps, misc = bank[0:2], bank[2], bank[3:5], bank[5], bank[6], bank[7]

        bdr_f = bdr[:, :, :, :].rearrange("p a t s -> p (a t s)")
        xn1 = bdr_f[:, 0:2 * S].rearrange("p (r t d) -> p r t d", r=2, t=T)
        xn2 = bdr_f[:, 2 * S:4 * S].rearrange("p (r t d) -> p r t d", r=2, t=T)
        x2T = bdr_f[:, 4 * S:6 * S].rearrange("p (r s) -> p r s", r=2)
        bdw_f = bdw[:, :, :, :].rearrange("p a t s -> p (a t s)")
        wstage = bdw_f[:, 0:2 * 2 * F].rearrange("p (r f) -> p r f", r=2)
        w2stage = bdw_f[:, 4 * F:4 * F + 2 * FT * D].rearrange("p (r f d) -> p r f d", r=2, f=FT)
        Sb_f = Sb[:, :, :].rearrange("p a s -> p (a s)")
        wq_sb, wk_sb, wv_sb, wp_sb = (Sb_f[:, i * D:(i + 1) * D] for i in range(4))
        pe_sb = Sb_f[:, 4 * D:4 * D + S]
        Pb_f = Pb[:, :, :].rearrange("p a s -> p (a s)")
        rows = Pb_f[0:7, 0:D]
        bv_bc = Pb_f[:, D:2 * D]
        bf_bc = Pb_f[:, 2 * D:3 * D]
        cols = Pb_f[:, 3 * D:3 * D + 8]
        wr_f = Pb_f[:, 3 * D + 8:3 * D + 8 + E]
        mv1 = Pb_f[:, 3 * D + 32:3 * D + 32 + 2 * T].rearrange("p (t k) -> p t k", k=2)
        mv2 = Pb_f[:, 3 * D + 48:3 * D + 48 + 2 * T].rearrange("p (t k) -> p t k", k=2)
        st6 = Pb_f[:, 3 * D + 64:3 * D + 64 + 6 * T].rearrange("p (t k) -> p t k", k=6)
        sd1 = Pb_f[:, 3 * D + 96:3 * D + 96 + T]
        sd2 = Pb_f[:, 3 * D + 104:3 * D + 104 + T]
        rd1 = Pb_f[:, 3 * D + 112:3 * D + 112 + T]
        rd2 = Pb_f[:, 3 * D + 120:3 * D + 120 + T]
        tri_sb = Pb_f[:, 4 * D:4 * D + E * E].rearrange("p (e j) -> p e j", j=E)
        BT = B * T
        lg = Pb_f[:, 5 * D:5 * D + BT * E].rearrange("p (i e) -> p i e", e=E)
        wr_h = qus[:, 0:E]
        wr_l = qus[:, E:2 * E]
        pT_h, pT_l = qvs[:, :], ks[:, :]
        PT_f = PTb[:, :, :].rearrange("p a s -> p (a s)")
        mx = PT_f[:, 0:BT]
        den = PT_f[:, 64:64 + BT]
        rden = PT_f[:, 128:128 + BT]
        rank = PT_f[:, 256:256 + BT * E].rearrange("p (i e) -> p i e", e=E)
        cmp1 = bdr_f[:, 0:BT * E * E].rearrange("p (i e j) -> p i e j", e=E, j=E)
        cmp2 = bdw_f[:, 0:BT * E * E].rearrange("p (i e j) -> p i e j", e=E, j=E)
        names = """c_in w_in0 w_in1 x_in w13_hi w13_lo w2_hi w2_lo
            rowsT cols_c cols_s wr_hi wr_lo p_mm p_hi p_lo p_rep p_all mask
            st ag ve sd rd nrm1 st2 ag2 ve2 sd2 rd2 nrm2 accd x1T xhi xlo x2Tm x2Tc qkv qu_hi qv_hi k_hi qu_lo qv_lo k_lo v_c lgm lgc
            route ex selq cwd
            zc qrep krep vrep qus_r ks_r qvs_r ps_r
            ac bd bdev ttr ex_d t te pv rsd oev x13 thd a_d h_d hhi hlo y accs
            met gath fT fTc fy fo""".split()
        s = {n: sem(n) for n in names}
        s_bdw = [sem("bd_written0"), sem("bd_written1")]
        s_bdr = [sem("bd_read0"), sem("bd_read1")]
        s_out = sem("out_written")
        s_w = [s["w_in0"], s["w_in1"]]
        NCONST = 17

        block = ctx.enter_context(nc.Block())

        def ge(eng, name, value):
            if isinstance(value, int) and value < 1:
                return
            eng.wait_ge(s[name] if isinstance(name, str) else name, value)

        def met(eng):
            eng.sem_inc(s["met"], 1)

        def hi_lo_terms(n):
            return [(0, 0), (0, 1), (1, 0), (1, 1)][:n]

        @block.sync
        def _(sp):
            sp.dma_start(acc[:, :, :, :].rearrange("p b t d -> p b (t d)"),
                         x.rearrange("b (p t) d -> p b (t d)", t=T)).then_inc(s["x_in"], 16)
            for r, a in enumerate((bq, bk, u, v, gamma, beta)):
                a1 = a.rearrange("h d -> (h d)") if len(a.shape) == 2 else a
                sp.dma_start(rows[r:r + 1, :], a1.rearrange("(a d) -> a d", a=1)).then_inc(s["c_in"], 16)
            sp.dma_start(rows[6:7, :], bq.rearrange("(a d) -> a d", a=1)).then_inc(s["c_in"], 16)
            for dst, a in ((wq_sb, Wq), (wk_sb, Wk), (wv_sb, Wv), (wp_sb, Wpos), (wf_sb[:, :], Wf), (wr_f, Wr),
                           (pe_sb, peT), (idf[:, :], ident), (selb[:, :, :, :, :], sel)):
                sp.dma_start(dst, a).then_inc(s["c_in"], 16)
            sp.dma_start(bv_bc, bv.partition_broadcast(P)).then_inc(s["c_in"], 16)
            sp.dma_start(bf_bc, bf.partition_broadcast(P)).then_inc(s["c_in"], 16)
            sp.dma_start(tri_sb.rearrange("p e j -> p (e j)"), tri.partition_broadcast(P)).then_inc(s["mask"], 16)
            for e in range(E):
                r = e % 2
                ge(sp, "w2_lo", e - 1)
                sp.dma_start(wstage[:, r, :], W13[e]).then_inc(s_w[r], 16)
                sp.dma_start(w2stage[:, r, 0:FT - 1, :],
                             W2[e, 0:(FT - 1) * P, :].rearrange("(f p) d -> p f d", p=P)).then_inc(s_w[r], 16)
                sp.dma_start(w2stage[0:FW[-1], r, FT - 1, :], W2[e, (FT - 1) * P:F, :]).then_inc(s_w[r], 16)

            def write_scores(n, g):
                ge(sp, "bdev", U * n + T * (g + 1))
                met(sp)
                if not isinstance(n, int) or n > 0:
                    ge(sp, s_bdr[g % 2], 16 * (2 * (n - 1) + g // 2 + 1))
                    met(sp)
                sp.dma_start(scratch[g].rearrange("(p w) -> p w", p=P),
                             bdw[:, g % 2, :, :].rearrange("p t s -> p (t s)")).then_inc(s_bdw[g % 2], 16)

            def read_scores(n, g):
                ge(sp, s_bdw[g % 2], 16 * (2 * n + g // 2 + 1))
                met(sp)
                ge(sp, "ttr", U * n + T * (g - 1))
                met(sp)
                sp.dma_start(bdr[:, g % 2, :, :].rearrange("p t s -> p (t s)"),
                             scratch[g, S:S * (S + 1)].rearrange("(p w) -> p w", p=P)).then_inc(s_bdr[g % 2], 16)

            ge(sp, "w2_lo", E)
            for g in range(GH):
                write_scores(0, g)
            ge(sp, "cwd", 1)
            for g in range(2):
                read_scores(0, g)

            def body(n, last):
                for g in range(GH):
                    if g < 2:
                        read_scores(n, g + 2)
                    elif not last:
                        read_scores(n + 1, g - 2)
                    if not last:
                        write_scores(n + 1, g)

            with sp.Fori(0, N - 1) as n:
                body(n, False)
            body(N - 1, True)

            with sp.Fori(0, B) as b:
                sp.wait_ge(s["fo"], b + 1)
                met(sp)
                sp.dma_start(out[ds(b, 1)].rearrange("a (p t) d -> p (a t d)", t=T),
                             acc[:, ds(b, 1), :, :].rearrange("p a t d -> p (a t d)")).then_inc(s_out, 16)
            sp.wait_ge(s_out, 16 * B)

        @block.gpsimd
        def _(pool):
            for e in range(E):
                r = e % 2
                pool.wait_ge(s_w[r], 48 * (e // 2 + 1))
                pool.tensor_copy(w13[:, 0, e, :], wstage[:, r, :]).then_inc(s["w13_hi"], 1)
                pool.tensor_copy(w2[:, 0, e, 0:FT - 1, :], w2stage[:, r, 0:FT - 1, :]).then_inc(s["w2_hi"], 1)
                pool.tensor_copy(w2[0:FW[-1], 0, e, FT - 1, :], w2stage[0:FW[-1], r, FT - 1, :]).then_inc(s["w2_hi"], 1)
                pool.wait_ge(s["w13_hi"], e + 1)
                pool.tensor_tensor(w13[:, 1, e, :], wstage[:, r, :], w13[:, 0, e, :], ALU.subtract).then_inc(s["w13_lo"], 1)
                pool.wait_ge(s["w2_hi"], 2 * e + 2)
                pool.tensor_tensor(w2[:, 1, e, 0:FT - 1, :], w2stage[:, r, 0:FT - 1, :], w2[:, 0, e, 0:FT - 1, :],
                                   ALU.subtract)
                pool.wait_ge(s["w13_lo"], e + 1)
                pool.tensor_tensor(w2[0:FW[-1], 1, e, FT - 1, :], w2stage[0:FW[-1], r, FT - 1, :],
                                   w2[0:FW[-1], 0, e, FT - 1, :], ALU.subtract).then_inc(s["w2_lo"], 1)
            for b in range(B):
                pool.wait_ge(s["nrm1"], b + 1)
                pool.tensor_tensor(acc[:, b, :, :], acc[:, b, :, :],
                                   bf_bc.unsqueeze(1).broadcast_to([P, T, D]), ALU.add).then_inc(s["accd"], 1)
            pool.wait_ge(s["cwd"], 1)
            pool.memset(bdw[:, :, :, 0:1], 0.0).then_inc(s["zc"], 1)

            def copy_p(n):
                ge(pool, "p_all", NG)
                if not isinstance(n, int) or n > 0:
                    ge(pool, "bd", U * n)
                met(pool)
                pool.tensor_copy(ps[:, :], pall[:, ds(n % NG, 1), :].rearrange("p a s -> p (a s)")).then_inc(s["ps_r"], 1)

            def split_hidden(n, su, f):
                j = NU * FT * n + FT * su + f
                w = FW[f]
                ge(pool, "h_d", j + 1)
                ge(pool, "y", T * (NU * n + su))
                met(pool)
                pool.tensor_copy(hh[0:w, f, :], hb[0:w, :]).then_inc(s["hhi"], 1)
                ge(pool, "hhi", j + 1)
                pool.tensor_tensor(hl[0:w, f, :], hb[0:w, :], hh[0:w, f, :], ALU.subtract).then_inc(s["hlo"], 1)

            def body(n, last):
                for i in range(U):
                    if i in HIDDEN_AT:
                        split_hidden(n, *HIDDEN_AT[i])
                if not last:
                    copy_p(n + 2)

            copy_p(0)
            copy_p(1)
            body(0, False)
            with pool.Fori(1, N - 2) as n:
                body(n, False)
            body(N - 2, True)
            body(N - 1, True)

            def gather_heads(b, r):
                pool.wait_ge(s["oev"], N)
                ge(pool, "fT", b - r)
                met(pool)
                dst = (Pb_f if r else Sb_f)[:, 0:T * D].rearrange("p (t n m) -> p n t m", t=T, n=NG)
                for n in range(NG):
                    src = vall[:, ds(b * NG + n, 1), :, :].rearrange("p a c m -> p (a c m)")
                    ins = pool.tensor_copy(dst[:, n].rearrange("p t (g d) -> p t g d", d=HD),
                                           src.rearrange("p (g t d) -> p t g d", g=GH, t=T))
                ins.then_inc(s["gath"], 1)

            gather_heads(0, 0)
            gather_heads(1, 1)
            with pool.Fori(1, B // 2) as i:
                for r in range(2):
                    gather_heads(2 * i + r, r)

        @block.scalar
        def _(act):
            act.wait_ge(s["rowsT"], 1)
            act.activation(cols[:, 0:6], misc[:, 0:6], ACT.Copy).then_inc(s["cols_c"], 1)
            act.wait_ge(s["p_mm"], 1)
            act.activation(pT_h, bank[2][:, :], ACT.Copy).then_inc(s["p_hi"], 1)
            for g in range(NG):
                act.wait_ge(s["p_rep"], g + 1)
                act.activation(pall[:, g, :], bank[3 + g % 2][:, :], ACT.Copy).then_inc(s["p_all"], 1)
            act.wait_ge(s["cols_s"], 2)
            def batch(b, r):
                act.wait_ge(s["ve"], b + 1)
                act.activation(sd1, sd1, ACT.Sqrt).then_inc(s["sd"], 1)
                act.wait_ge(s["ve2"], b + 1)
                act.activation(sd2, sd2, ACT.Sqrt).then_inc(s["sd2"], 1)
                act.wait_ge(s["x1T"], b + 1)
                act.activation(xnT[:, 0, ds(b, 1), :].rearrange("p a s -> p (a s)"), bank[0][:, :],
                               ACT.Copy).then_inc(s["xhi"], 1)
                act.wait_ge(s["x2Tm"], b + 1)
                act.activation(x2T[:, r, :].rearrange("p (q t) -> p q t", t=T),
                               bank[1][:, :].rearrange("p (t q) -> p q t", t=T),
                               ACT.Identity, bias=cols[:, 5:6], scale=cols[:, 4:5]).then_inc(s["x2Tc"], 1)
                act.wait_ge(s["qkv"], 3 * b + 1)
                act.activation(quT[:, 0, ds(b, 1), :].rearrange("p a s -> p (a s)"), bank[3][:, :], ACT.Identity,
                               bias=cols[:, 6:7]).then_inc(s["qu_hi"], 1)
                act.activation(qvT[:, 0, ds(b, 1), :].rearrange("p a s -> p (a s)"), bank[3][:, :], ACT.Identity,
                               bias=cols[:, 7:8]).then_inc(s["qv_hi"], 1)
                act.wait_ge(s["qkv"], 3 * b + 2)
                act.activation(kT[:, 0, ds(b, 1), :].rearrange("p a s -> p (a s)"), bank[4][:, :], ACT.Identity,
                               bias=cols[:, 1:2]).then_inc(s["k_hi"], 1)

            batch(0, 0)
            batch(1, 1)
            with act.Fori(1, B // 2) as i:
                for r in range(2):
                    batch(2 * i + r, r)
            act.wait_ge(s["route"], 1)
            act.activation(lg, lg, ACT.Exp).then_inc(s["ex"], 1)

            def evac_qv(n):
                ge(act, "qrep", n + 1)
                act.activation(qvs[:, :].rearrange("p (t q) -> p t q", t=T),
                               bd_ps[:, :].rearrange("p (q t) -> p t q", t=T), ACT.Copy).then_inc(s["qvs_r"], 1)

            def evac_k(n):
                ge(act, "krep", n + 1)
                act.activation(ks[:, :], x3_ps[:, :], ACT.Copy).then_inc(s["ks_r"], 1)

            def evac_scores(n, i):
                g, t = divmod(i, T)
                if t == 0:
                    ge(act, s_bdw[g % 2], 16 * (2 * n + g // 2))
                ge(act, "bd", U * n + i + 1)
                act.activation(bdw[:, g % 2, t, 1:S + 1], bd_ps[:, :], ACT.Copy).then_inc(s["bdev"], 1)

            def softmax_exp(n, i):
                k = U * n + i
                ge(act, "ttr", k + 1)
                ge(act, "t", k - 1)
                act.activation(Pb[:, i % 2, :], Sb[:, i % 2, :], ACT.Exp, bias=nmax[:, i:i + 1], scale=-1.0,
                               accum_out=sums[:, ds(n, 1), i:i + 1].rearrange("p a b -> p (a b)")).then_inc(s["ex_d"], 1)

            def gate(n, su, f):
                j = NU * FT * n + FT * su + f
                w = FW[f]
                ge(act, "x13", j + 1)
                ge(act, "a_d", j)
                act.activation(th[0:w, :], x1_ps[0:w, :], ACT.Tanh, scale=0.5).then_inc(s["thd"], 1)

            def body(n, last):
                for i in range(U):
                    if not last:
                        evac_scores(n + 1, i)
                    softmax_exp(n, i)
                    if i in HIDDEN_AT:
                        gate(n, *HIDDEN_AT[i])
                if not last:
                    evac_k(n + 1)

            act.wait_ge(s["zc"], 1)
            evac_qv(0)
            for i in range(U):
                evac_scores(0, i)
            evac_k(0)
            evac_qv(1)
            body(0, False)
            with act.Fori(1, N - 1) as n:
                evac_qv(n + 1)
                body(n, False)
            body(N - 1, True)
            def evac_heads(b, r):
                ge(act, "fT", b + 1)
                ge(act, "fy", b - r)
                act.activation(PTb[:, r, :], bank[0][:, :], ACT.Copy).then_inc(s["fTc"], 1)

            evac_heads(0, 0)
            evac_heads(1, 1)
            with act.Fori(1, B // 2) as i:
                for r in range(2):
                    evac_heads(2 * i + r, r)

        @block.tensor
        def _(pe):
            pe.wait_ge(s["c_in"], 16 * 18)
            pe.transpose(misc[:, 0:7], rows, idf[0:7, 0:7]).then_inc(s["rowsT"], 1)
            pe.matmul(bank[2][:, :], wp_sb, pe_sb, start=True, stop=True).then_inc(s["p_mm"], 1)
            pe.wait_ge(s["p_hi"], 1)
            pe.wait_ge(s["p_lo"], 1)
            for g in range(NG):
                ge(pe, "p_all", g - 1)
                for part, src in enumerate((pT_h, pT_l)):
                    mm = pe.matmul(bank[3 + g % 2][:, :], selb[:, 1, part, g, :], src, start=(part == 0), stop=(part == 1))
                mm.then_inc(s["p_rep"], 1)
            pe.wait_ge(s["p_all"], NG)
            pe.wait_ge(s["wr_lo"], 1)
            def batch(b, r):
                pe.wait_ge(s["nrm1"], b + 1)
                ge(pe, "xlo", b)
                for t in range(T):
                    mm = pe.transpose(bank[0][:, t * P:(t + 1) * P], xn1[:, r, t, :],
                                      idf[:, :])
                mm.then_inc(s["x1T"], 1)
                pe.wait_ge(s["nrm2"], b + 1)
                ge(pe, "x2Tc", b)
                for t in range(T):
                    mm = pe.transpose(bank[1][:, t * P:(t + 1) * P], xn2[:, r, t, :],
                                      idf[:, :])
                mm.then_inc(s["x2Tm"], 1)
                pe.wait_ge(s["x2Tc"], b + 1)
                xt = x2T[:, r, :]
                ge(pe, "qv_lo", b)
                pe.matmul(bank[3][:, :], wq_sb, xt, start=True, stop=True).then_inc(s["qkv"], 1)
                ge(pe, "k_lo", b)
                pe.matmul(bank[4][:, :], wk_sb, xt, start=True, stop=True).then_inc(s["qkv"], 1)
                ge(pe, "v_c", b)
                for c in range(T):
                    mm = pe.matmul(bank[5][:, c * D:(c + 1) * D],
                                   x2T[:, r, c * P:(c + 1) * P], wv_sb, start=True, stop=True)
                mm.then_inc(s["qkv"], 1)
                pe.wait_ge(s["xlo"], b + 1)
                terms = hi_lo_terms(4)
                for t in range(T):
                    for m, (a, w) in enumerate(terms):
                        mm = pe.matmul(misc[:, ds((b * T + t) * E, E)],
                                       xnT[:, a, ds(b, 1), t * P:(t + 1) * P].rearrange("p a s -> p (a s)"),
                                       wr_l if w else wr_h, start=(m == 0), stop=(m == 3))
                mm.then_inc(s["lgm"], 1)

            batch(0, 0)
            batch(1, 1)
            with pe.Fori(1, B // 2) as i:
                for r in range(2):
                    batch(2 * i + r, r)
            pe.wait_ge(s["lgc"], 1)
            pe.wait_ge(s["v_c"], B)
            pe.wait_ge(s["k_lo"], B)
            pe.wait_ge(s["qv_lo"], B)
            pe.wait_ge(s["w2_lo"], E)

            def replicate(dst, src, pattern, n):
                for part in range(2):
                    mm = pe.matmul(dst[:, :], selb[:, pattern, part, ds(n % NG, 1), :].rearrange("p a m -> p (a m)"),
                                   src[:, part, ds(n // NG, 1), :].rearrange("p a s -> p (a s)"),
                                   start=(part == 0), stop=(part == 1))
                return mm

            def rep_qv(n):
                if not isinstance(n, int) or n > 0:
                    ge(pe, "bdev", U * n)
                replicate(bd_ps, qvT, 0, n).then_inc(s["qrep"], 1)

            def rep_qu_k(n):
                if not isinstance(n, int) or n > 0:
                    ge(pe, "h_d", NU * FT * n)
                    ge(pe, "accs", NU * T * n)
                replicate(x1_ps, quT, 0, n).then_inc(s["vrep"], 1)
                replicate(x3_ps, kT, 1, n).then_inc(s["krep"], 1)

            def position_scores(n, i):
                g, t = divmod(i, T)
                if i == 0:
                    ge(pe, "qvs_r", n + 1)
                    ge(pe, "ps_r", n + 1)
                ge(pe, "bdev", U * n + i)
                r = slice(SLOT * g, SLOT * (g + 1))
                pe.matmul(bd_ps[:, :], qvs[r, t * P:(t + 1) * P], ps[r, :], start=True, stop=True).then_inc(s["bd"], 1)

            def content_scores(n, i):
                g, t = divmod(i, T)
                if i == 0:
                    ge(pe, "qus_r", n + 1)
                    ge(pe, "ks_r", n + 1)
                ge(pe, "ttr", U * n + i - 1)
                r = slice(SLOT * g, SLOT * (g + 1))
                pe.matmul(ac_ps[i % 2][:, :], qus[r, t * P:(t + 1) * P], ks[r, :], start=True, stop=True).then_inc(s["ac"], 1)

            def transposes(n, i):
                k = U * n + i
                ge(pe, "ex_d", k + 1)
                ge(pe, "te", k - 1)
                for c in range(T):
                    mm = pe.transpose(tp_ps[i % 2][:, c * P:(c + 1) * P], Pb[:, i % 2, c * P:(c + 1) * P], idf[:, :])
                mm.then_inc(s["t"], 1)

            def weighted_v(n, i):
                g, t = divmod(i, T)
                k = U * n + i
                ge(pe, "te", k + 1)
                if i == 0:
                    ge(pe, "oev", n)
                for c in range(T):
                    mm = pe.matmul(misc[:, i * HD:(i + 1) * HD], PTb[:, i % 2, c * P:(c + 1) * P],
                                   vall[:, ds(n, 1), c, g * HD:(g + 1) * HD].rearrange("p a d -> p (a d)"),
                                   start=(c == 0), stop=(c == T - 1))
                mm.then_inc(s["pv"], 1)

            def hidden(n, su, f):
                j = NU * FT * n + FT * su + f
                w = FW[f]
                ge(pe, "h_d", j)
                if f == 0:
                    ge(pe, "accs", T * (NU * n + su))
                e, b = n // NG, NU * (n % NG) + su
                for dst, o in ((x1_ps, 0), (x3_ps, F)):
                    for m, (wp, xp) in enumerate(hi_lo_terms(3)):
                        mm = pe.matmul(dst[0:w, :],
                                       w13[:, wp, ds(e, 1), o + P * f:o + P * f + w].rearrange("p a m -> p (a m)"),
                                       xnT[:, xp, ds(b, 1), :].rearrange("p a s -> p (a s)"),
                                       start=(m == 0), stop=(m == 2))
                mm.then_inc(s["x13"], 1)

            def down(n, su, t):
                y = T * (NU * n + su) + t
                e = n // NG
                if t == 0:
                    ge(pe, "hlo", FT * (NU * n + su) + FT)
                o = t * D
                steps = [(f, hp, wp) for f in range(FT) for hp, wp in hi_lo_terms(3)]
                for m, (f, hp, wp) in enumerate(steps):
                    w = FW[f]
                    h = (hl if hp else hh)[0:w, f, t * P:(t + 1) * P]
                    mm = pe.matmul(x1_ps[:, o:o + D], h, w2[0:w, wp, ds(e, 1), f, :].rearrange("p a d -> p (a d)"),
                                   start=(m == 0), stop=(m == len(steps) - 1))
                mm.then_inc(s["y"], 1)

            def body(n, first, last):
                for i in range(U):
                    content_scores(n, i)
                    if not last:
                        position_scores(n + 1, i)
                    if i >= 2:
                        transposes(n, i - 2)
                    elif not first:
                        transposes(n - 1, U + i - 2)
                    if i >= 3:
                        weighted_v(n, i - 3)
                    elif not first:
                        weighted_v(n - 1, U + i - 3)
                    if i in HIDDEN_AT:
                        hidden(n, *HIDDEN_AT[i])
                    for su, t in DOWN_AT.get(i, []):
                        down(n, su, t)
                if not last:
                    rep_qu_k(n + 1)

            rep_qv(0)
            for i in range(U):
                position_scores(0, i)
            rep_qu_k(0)
            rep_qv(1)
            body(0, True, False)
            with pe.Fori(1, N - 1) as n:
                rep_qv(n + 1)
                body(n, False, False)
            body(N - 1, False, True)
            transposes(N - 1, U - 2)
            weighted_v(N - 1, U - 3)
            transposes(N - 1, U - 1)
            weighted_v(N - 1, U - 2)
            weighted_v(N - 1, U - 1)

            pe.wait_ge(s["oev"], N)
            pe.wait_ge(s["accs"], N * NU * T)
            def project(b, r):
                pe.wait_ge(s["gath"], b + 1)
                ge(pe, "fTc", b)
                for t in range(T):
                    mm = pe.transpose(bank[0][:, t * P:(t + 1) * P], Sb_f[:, t * D:(t + 1) * D] if r == 0 else
                                      Pb_f[:, t * D:(t + 1) * D], idf[:, :])
                mm.then_inc(s["fT"], 1)
                pe.wait_ge(s["fTc"], b + 1)
                ge(pe, "fo", b)
                for t in range(T):
                    mm = pe.matmul(bank[2][:, t * D:(t + 1) * D], PTb[:, r, t * P:(t + 1) * P], wf_sb[:, :],
                                   start=True, stop=True)
                mm.then_inc(s["fy"], 1)

            project(0, 0)
            project(1, 1)
            with pe.Fori(1, B // 2) as i:
                for r in range(2):
                    project(2 * i + r, r)


        @block.vector
        def _(dve):
            V = nc.vector
            dve.wait_ge(s["cols_c"], 1)
            V.tensor_tensor(cols[:, 6:7], cols[:, 0:1], cols[:, 2:3], ALU.add).then_inc(s["cols_s"], 1)
            V.tensor_tensor(cols[:, 7:8], cols[:, 0:1], cols[:, 3:4], ALU.add).then_inc(s["cols_s"], 1)
            V.tensor_copy(wr_h, wr_f).then_inc(s["wr_hi"], 1)
            dve.wait_ge(s["wr_hi"], 1)
            V.tensor_tensor(wr_l, wr_f, wr_h, ALU.subtract).then_inc(s["wr_lo"], 1)
            dve.wait_ge(s["p_hi"], 1)
            V.tensor_tensor(pT_l, bank[2][:, :], pT_h, ALU.subtract).then_inc(s["p_lo"], 1)
            dve.wait_ge(s["cols_s"], 2)
            dve.wait_ge(s["x_in"], 16)

            def norm_rows(b, src, dst, mv, sd, rd, s_st, s_ag, s_ve, s_sd, s_rd, s_nrm):
                ge(dve, s_ag, T * b)
                for t in range(T):
                    V.bn_stats(st6[:, t, :], src(t)).then_inc(s[s_st], 1)
                for t in range(T):
                    dve.wait_ge(s[s_st], T * b + t + 1)
                    met(dve)
                    V.bn_aggr(mv[:, t, :], st6[:, t, :]).then_inc(s[s_ag], 1)
                dve.wait_ge(s[s_ag], T * (b + 1))
                V.tensor_scalar(sd, mv[:, :, 1], EPS, None, ALU.add).then_inc(s[s_ve], 1)
                dve.wait_ge(s[s_sd], b + 1)
                V.reciprocal(rd, sd).then_inc(s[s_rd], 1)
                dve.wait_ge(s[s_rd], b + 1)
                for t in range(T):
                    ins = V.tensor_scalar(dst(t), src(t), mv[:, t, 0:1], rd[:, t:t + 1], ALU.subtract, ALU.mult)
                ins.then_inc(s[s_nrm], 1)

            def batch(b, ring):
                def tile_of(a, r):
                    return lambda t: a[:, r, t, :] if isinstance(r, int) else \
                        a[:, ds(r, 1), t, :].rearrange("p a d -> p (a d)")
                norm_rows(b, tile_of(acc, b), tile_of(xn1, ring), mv1, sd1, rd1, "st", "ag", "ve", "sd", "rd", "nrm1")
                dve.wait_ge(s["nrm1"], b + 1)
                norm_rows(b, tile_of(xn1, ring), tile_of(xn2, ring), mv2, sd2, rd2, "st2", "ag2", "ve2", "sd2", "rd2",
                          "nrm2")

                def low(name, dst, src, hi, bias, after, count):
                    dve.wait_ge(s[after], count)
                    one = lambda a: a[:, ds(b, 1), :].rearrange("p a s -> p (a s)")
                    if bias is None:
                        V.tensor_tensor(one(dst), src, one(hi), ALU.subtract).then_inc(s[name], 1)
                    else:
                        V.scalar_tensor_tensor(out=one(dst), in0=src, scalar=bias, in1=one(hi), op0=ALU.add,
                                               op1=ALU.subtract).then_inc(s[name], 1)

                low("xlo", xnT[:, 1], bank[0][:, :], xnT[:, 0], None, "xhi", b + 1)
                low("qu_lo", quT[:, 1], bank[3][:, :], quT[:, 0], cols[:, 6:7], "qv_hi", b + 1)
                low("qv_lo", qvT[:, 1], bank[3][:, :], qvT[:, 0], cols[:, 7:8], "qv_hi", b + 1)
                low("k_lo", kT[:, 1], bank[4][:, :], kT[:, 0], cols[:, 1:2], "k_hi", b + 1)
                dve.wait_ge(s["qkv"], 3 * b + 3)
                for c in range(T):
                    ins = V.tensor_tensor(vall[:, ds(b * NG, NG), c, :],
                                          bank[5][:, c * D:(c + 1) * D].rearrange("p (n m) -> p n m", n=NG),
                                          bv_bc.rearrange("p (n m) -> p n m", n=NG), ALU.add)
                ins.then_inc(s["v_c"], 1)

            batch(0, 0)
            batch(1, 1)
            with dve.Fori(1, B // 2) as i:
                for r in range(2):
                    batch(2 * i + r, r)

            chain = [0]

            def step(ins):
                ins.then_inc(s["selq"], 1)
                chain[0] += 1
                dve.wait_ge(s["selq"], chain[0])

            dve.wait_ge(s["lgm"], B)
            dve.wait_ge(s["mask"], 16)
            V.tensor_copy(lg, misc[:, 0:BT * E].rearrange("p (i e) -> p i e", e=E)).then_inc(s["lgc"], 1)
            dve.wait_ge(s["lgc"], 1)
            step(V.tensor_reduce(mx, lg, AX.X, ALU.max))
            V.tensor_tensor(lg, lg, mx.unsqueeze(2).broadcast_to([P, BT, E]), ALU.subtract).then_inc(s["route"], 1)
            dve.wait_ge(s["ex"], 1)
            dve.wait_ge(s["w2_lo"], E)
            pj = lg.unsqueeze(2).broadcast_to([P, BT, E, E])
            pi = lg.unsqueeze(3).broadcast_to([P, BT, E, E])
            step(V.tensor_tensor(cmp1, pj, pi, ALU.is_gt))
            step(V.tensor_tensor(cmp2, pj, pi, ALU.is_equal))
            step(V.tensor_tensor(cmp2, cmp2, tri_sb.unsqueeze(1).broadcast_to([P, BT, E, E]), ALU.mult))
            step(V.tensor_tensor(cmp1, cmp1, cmp2, ALU.add))
            step(V.tensor_reduce(rank, cmp1, AX.X, ALU.add))
            step(V.tensor_scalar(rank, rank, float(TOPK), 0.5, ALU.is_lt, ALU.mult))
            step(V.tensor_tensor(rank, rank, lg, ALU.mult))
            step(V.tensor_reduce(den, rank, AX.X, ALU.add))
            step(V.tensor_scalar(den, den, 2.0, None, ALU.mult))
            step(V.reciprocal(rden, den))
            V.tensor_tensor(cw[:, :, :], rank, rden.unsqueeze(2).broadcast_to([P, BT, E]), ALU.mult).then_inc(s["cwd"], 1)
            dve.wait_ge(s["accd"], B)
            dve.wait_ge(s["cwd"], 1)

            def evac_qu(n):
                ge(dve, "vrep", n + 1)
                V.tensor_copy(qus[:, :].rearrange("p (t q) -> p t q", t=T),
                              x1_ps[:, :].rearrange("p (q t) -> p t q", t=T)).then_inc(s["qus_r"], 1)

            def add_scores(n, i):
                g, t = divmod(i, T)
                k = U * n + i
                ge(dve, "ac", k + 1)
                if t == 0:
                    ge(dve, s_bdr[g % 2], 16 * (2 * n + g // 2 + 1))
                ge(dve, "ex_d", k - 1)
                met(dve)
                V.tensor_tensor_reduce(out=Sb[:, i % 2, :], in0=ac_ps[i % 2][:, :], in1=bdr[:, g % 2, t, :],
                                       scale=-SCALE, scalar=3.0e38, op0=ALU.add, op1=ALU.min,
                                       accum_out=nmax[:, i:i + 1]).then_inc(s["ttr"], 1)

            def evac_T(n, i):
                k = U * n + i
                ge(dve, "t", k + 1)
                ge(dve, "pv", k - 1)
                V.tensor_copy(PTb[:, i % 2, :], tp_ps[i % 2][:, :]).then_inc(s["te"], 1)

            def evac_out(n):
                ge(dve, "pv", U * (n + 1))
                V.reciprocal(rs[:, :], sums[:, ds(n, 1), :].rearrange("p a i -> p (a i)")).then_inc(s["rsd"], 1)
                ge(dve, "rsd", n + 1)
                V.tensor_tensor(vall[:, ds(n, 1), :, :].rearrange("p a c m -> p (a c m)").rearrange("p (i d) -> p i d", d=HD),
                                misc[:, 0:U * HD].rearrange("p (i d) -> p i d", d=HD),
                                rs[:, :].unsqueeze(2).broadcast_to([P, U, HD]), ALU.mult).then_inc(s["oev"], 1)

            def hidden(n, su, f):
                j = NU * FT * n + FT * su + f
                w = FW[f]
                ge(dve, "thd", j + 1)
                V.scalar_tensor_tensor(out=ab[0:w, :], in0=th[0:w, :], scalar=1.0, in1=x1_ps[0:w, :], op0=ALU.add,
                                       op1=ALU.mult).then_inc(s["a_d"], 1)
                ge(dve, "a_d", j + 1)
                ge(dve, "hlo", j)
                V.tensor_tensor(hb[0:w, :], ab[0:w, :], x3_ps[0:w, :], ALU.mult).then_inc(s["h_d"], 1)

            def add_expert(n, su, t):
                y = T * (NU * n + su) + t
                e, b = n // NG, NU * (n % NG) + su
                ge(dve, "y", T * (NU * n + su + 1))
                ge(dve, "accs", y)
                a = acc[:, ds(b, 1), t, :].rearrange("p a d -> p (a d)")
                V.scalar_tensor_tensor(out=a, in0=x1_ps[:, t * D:(t + 1) * D],
                                       scalar=cw[:, ds(b * T + t, 1), ds(e, 1)].rearrange("p a e -> p (a e)"),
                                       in1=a, op0=ALU.mult, op1=ALU.add).then_inc(s["accs"], 1)

            def body(n, first, last):
                for i in range(U + 1):
                    if i < U:
                        add_scores(n, i)
                        if i >= 2:
                            evac_T(n, i - 2)
                        elif not first:
                            evac_T(n - 1, U + i - 2)
                        if i == 3 and not first:
                            evac_out(n - 1)
                    if i - 1 in HIDDEN_AT:
                        hidden(n, *HIDDEN_AT[i - 1])
                    for su, t in DOWN_AT.get(i - 1, []):
                        if t == T - 1:
                            for tt in range(T):
                                add_expert(n, su, tt)
                if not last:
                    evac_qu(n + 1)

            evac_qu(0)
            body(0, True, False)
            with dve.Fori(1, N - 1) as n:
                body(n, False, False)
            body(N - 1, False, True)
            evac_T(N - 1, U - 2)
            evac_T(N - 1, U - 1)
            evac_out(N - 1)

            with dve.Fori(0, B) as b:
                dve.wait_ge(s["fy"], b + 1)
                a = acc[:, ds(b, 1), :, :].rearrange("p a t d -> p (a t d)")
                V.tensor_tensor(a, a, bank[2][:, :], ALU.add).then_inc(s["fo"], 1)


_INS = ['L0_attn_x', 'L0_attn_Wq', 'L0_attn_bq', 'L0_attn_Wk', 'L0_attn_bk', 'L0_attn_Wv', 'L0_attn_bv',
        'L0_attn_Wpos', 'L0_attn_Wf', 'L0_attn_bf', 'L0_attn_u', 'L0_attn_v', 'L0_attn_gamma', 'L0_attn_beta',
        'L0_ffn_W13', 'L0_ffn_W2', 'L0_ffn_Wr']


def shape_constants(S, D, H, HD, E):
    import numpy as np

    pos = np.arange(S, dtype=np.float32)
    inv_freq = (np.float32(1.0) / np.power(np.float32(10000.0), np.arange(0.0, D, 2.0, dtype=np.float32) / np.float32(D)))
    angles = pos[:, None] * inv_freq[None, :].astype(np.float32)
    pe = np.zeros((S, D), np.float32)
    pe[:, 0::2] = np.sin(angles)
    pe[:, 1::2] = np.cos(angles)
    sel = np.zeros((H, HD, 2, 2, H // 4, 4, 4, HD), np.float16)
    for h in range(H):
        for d in range(HD):
            for pattern, parts in enumerate(((0, 0, 1, 1), (0, 1, 0, 1))):
                for copy, part in enumerate(parts):
                    sel[h, d, pattern, part, h // 4, h % 4, copy, d] = 1.0
    tri = np.tril(np.ones((E, E), np.float32), -1)
    return {
        "peT": np.ascontiguousarray(pe.T), "ident": np.eye(128, dtype=np.float32),
        "sel": sel.reshape(H * HD, 2, 2, H // 4, 128), "tri": tri.reshape(-1),
    }


def kernel(**inputs):
    import numpy as _np
    import concourse.bacc as _bacc
    from concourse import mybir as _mybir
    from concourse.bass_utils import run_bass_kernel_spmd as _run

    nc = _bacc.Bacc("TRN2", target_bir_lowering=False, num_devices=1)
    arrays, args = {}, []
    given = {n: _np.ascontiguousarray(inputs[n]) for n in _INS}
    B, S, D = given['L0_attn_x'].shape
    H, HD = given['L0_attn_u'].shape
    E = given['L0_ffn_Wr'].shape[1]
    given.update(shape_constants(S, D, H, HD, E))
    for name, a in given.items():
        arrays[f"in_{name}_dram"] = a
        args.append(nc.dram_tensor(f"in_{name}_dram", a.shape, _mybir.dt.from_np(a.dtype), kind="ExternalInput").ap())
    args.append(nc.dram_tensor("out_0_dram", (B, S, D), F32, kind="ExternalOutput").ap())
    build(nc, *args)
    r = _run(nc, [arrays], core_ids=[0])
    return r.results[0]["out_0_dram"]
```

```python
from contextlib import ExitStack

import concourse.bass as bass
from concourse import mybir

ALU = mybir.AluOpType
ACT = mybir.ActivationFunctionType
AX = mybir.AxisListType
F32 = mybir.dt.float32
F16 = mybir.dt.float16
ds = bass.ds

P = 128
EPS = 1e-5
TOPK = 2


def build(nc, x, Wq, bq, Wk, bk, Wv, bv, Wpos, Wf, bf, u, v, gamma, beta, W13, W2, Wr, peT, ident, sel, tri, out):
    B, S, D = x.shape
    H, HD = u.shape
    E, F, _ = W2.shape
    T = S // P
    GH = 4
    NG = H // GH
    N = B * NG
    U = GH * T
    FT = -(-F // P)
    FW = [min(P, F - P * f) for f in range(FT)]
    NU = B * E // N
    SCALE = 1.0 / float(D) ** 0.5
    SLOT = P // GH
    assert D == P and S == T * P and SLOT == 4 * HD and NU == 2 and E == 8 and NG == 4

    HIDDEN_AT = {1: (0, 0), 3: (0, 1), 5: (0, 2), 7: (1, 0), 10: (1, 1), 12: (1, 2)}
    DOWN_AT = {0: (1, (0, 1)), 1: (1, (2, 3)), 8: (0, (0, 1)), 9: (0, (2, 3))}

    with ExitStack() as ctx:
        def sb(name, shape, dt=F32):
            return ctx.enter_context(nc.sbuf_tensor(name, shape, dt))

        def sem(name):
            return ctx.enter_context(nc.semaphore(name))

        scratch = nc.dram_tensor("scratch", [GH, S * (S + 1)], F32).ap()

        acc = sb("acc", [P, B, T, D])
        xnT = sb("xnT", [P, 2, B, S], F16)
        quT = sb("quT", [P, 2, B, S], F16)
        qvT = sb("qvT", [P, 2, B, S], F16)
        kT = sb("kT", [P, 2, B, S], F16)
        heads = sb("heads", [P, N, U * HD])
        vv = heads[:, :, :].bitcast(F16).rearrange("p n (c g k d) -> p n c g k d", c=T, g=GH, k=2)
        w13 = sb("w13", [P, 2, E, 2 * F], F16)
        w2 = sb("w2", [P, 2, E, FT, D], F16)
        pall = sb("pall", [P, NG, S], F16)
        idf = sb("idf", [P, P])
        selb = sb("selb", [P, 2, 2, NG, P], F16)
        cw = sb("cw", [P, B * T, E])
        wf_sb = sb("wf_sb", [P, D])
        sums = sb("sums", [P, 2, U])
        rs = sb("rs", [P, U])
        nmax = sb("nmax", [P, U])
        bdr = sb("bdr", [P, GH, T, S])
        bdw = sb("bdw", [P, 2, T, S + 1])
        qus = sb("qus", [P, S], F16)
        qvs = sb("qvs", [P, S], F16)
        ks = sb("ks", [P, S], F16)
        ps = sb("ps", [P, S], F16)
        PTh = sb("PTh", [P, 2, S], F16)
        PTl = sb("PTl", [P, 2, S], F16)
        tmp = sb("tmp", [P, U, HD])
        ob = sb("ob", [P, U * 2 * HD])
        hb = sb("hb", [P, 2, S])
        hh = sb("hh", [P, FT, S], F16)
        hl = sb("hl", [P, FT, S], F16)

        bank = [ctx.enter_context(nc.psum_tensor(f"bank{i}", [P, 512], F32)) for i in range(8)]
        ac_ps, y_ps, bd_ps, tp_ps, x1_ps, x3_ps, misc = bank[0], bank[1], bank[2], bank[3:5], bank[5], bank[6], bank[7]

        bdr_f = bdr[:, :, :, :].rearrange("p a t s -> p (a t s)")
        xn1 = bdr_f[:, 0:2 * S].rearrange("p (r t d) -> p r t d", r=2, t=T)
        xn2 = bdr_f[:, 2 * S:4 * S].rearrange("p (r t d) -> p r t d", r=2, t=T)
        x2T = bdr_f[:, 4 * S:6 * S].rearrange("p (r s) -> p r s", r=2)
        bdw_f = bdw[:, :, :, :].rearrange("p a t s -> p (a t s)")
        wstage = bdw_f[:, 0:2 * 2 * F].rearrange("p (r f) -> p r f", r=2)
        w2stage = bdw_f[:, 4 * F:4 * F + 2 * FT * D].rearrange("p (r f d) -> p r f d", r=2, f=FT)
        Sb_f = bdr_f[:, 6 * S:8 * S]
        wq_sb, wk_sb, wv_sb, wp_sb = (Sb_f[:, i * D:(i + 1) * D] for i in range(4))
        pe_sb = Sb_f[:, 4 * D:4 * D + S]
        Pb_f = bdr_f[:, 8 * S:10 * S]
        rows = Pb_f[0:7, 0:D]
        bv_bc = Pb_f[:, D:2 * D]
        bf_bc = Pb_f[:, 2 * D:3 * D]
        cols = Pb_f[:, 3 * D:3 * D + 8]
        wr_f = Pb_f[:, 3 * D + 8:3 * D + 8 + E]
        mv1 = Pb_f[:, 3 * D + 32:3 * D + 32 + 2 * T].rearrange("p (t k) -> p t k", k=2)
        mv2 = Pb_f[:, 3 * D + 48:3 * D + 48 + 2 * T].rearrange("p (t k) -> p t k", k=2)
        st6 = Pb_f[:, 3 * D + 64:3 * D + 64 + 6 * T].rearrange("p (t k) -> p t k", k=6)
        sd1 = Pb_f[:, 3 * D + 96:3 * D + 96 + T]
        sd2 = Pb_f[:, 3 * D + 104:3 * D + 104 + T]
        rd1 = Pb_f[:, 3 * D + 112:3 * D + 112 + T]
        rd2 = Pb_f[:, 3 * D + 120:3 * D + 120 + T]
        tri_sb = Pb_f[:, 4 * D:4 * D + E * E].rearrange("p (e j) -> p e j", j=E)
        BT = B * T
        lg = Pb_f[:, 5 * D:5 * D + BT * E].rearrange("p (i e) -> p i e", e=E)
        wr_h = qus[:, 0:E]
        wr_l = qus[:, E:2 * E]
        pT_h, pT_l = qvs[:, :], ks[:, :]
        mx = hb[:, 0, 0:BT]
        den = hb[:, 0, 64:64 + BT]
        rden = hb[:, 0, 128:128 + BT]
        rank = hb[:, 1, 0:BT * E].rearrange("p (i e) -> p i e", e=E)
        cmp1 = bdr_f[:, 0:BT * E * E].rearrange("p (i e j) -> p i e j", e=E, j=E)
        cmp2 = bdw_f[:, 0:BT * E * E].rearrange("p (i e j) -> p i e j", e=E, j=E)
        aT = bdr[:, 0, 0:2, :]

        def j_ring(su, f):
            return (FT * su + f) % 2

        def v_part(b, c, k):
            return vv[:, ds(b * NG, NG), c, :, k, :] if not isinstance(b, int) else vv[:, b * NG:(b + 1) * NG, c, :, k, :]

        def v_rows(c):
            return hb[:, 0, c * D:(c + 1) * D].rearrange("p (n g d) -> p n g d", n=NG, g=GH)

        RA = 3
        LT, LL, LV = 2, 3, 4

        names = """v_hi v_lo thi oc ou c_in w_in0 w_in1 x_in w13_hi w13_lo w2_hi w2_lo
            rowsT cols_c cols_s wr_hi wr_lo p_mm p_hi p_lo p_rep p_all mask
            st ag ve sd rd nrm1 st2 ag2 ve2 sd2 rd2 nrm2 accd x1T xhi xlo x2Tm x2Tc qkv qu_hi qv_hi k_hi qu_lo qv_lo k_lo v_c lgm lgc
            route ex selq cwd
            zc qrep krep vrep qus_r ks_r qvs_r ps_r
            ac bd bdev ttr ex_d t te pv rsd oev x13 thd a_d h_d hhi hlo y accs
            met gath fT fTc fy fo""".split()
        s = {n: sem(n) for n in names}
        s_bdw = [sem("bd_written0"), sem("bd_written1")]
        s_bdr = [sem(f"bd_read{g}") for g in range(GH)]
        s_out = sem("out_written")
        s_w = [s["w_in0"], s["w_in1"]]
        NCONST = 17

        block = ctx.enter_context(nc.Block())

        def ge(eng, name, value):
            if isinstance(value, int) and value < 1:
                return
            eng.wait_ge(s[name] if isinstance(name, str) else name, value)

        def met(eng):
            eng.sem_inc(s["met"], 1)

        def hi_lo_terms(n):
            return [(0, 0), (0, 1), (1, 0), (1, 1)][:n]

        @block.sync
        def _(sp):
            sp.dma_start(acc[:, :, :, :].rearrange("p b t d -> p b (t d)"),
                         x.rearrange("b (p t) d -> p b (t d)", t=T)).then_inc(s["x_in"], 16)
            for r, a in enumerate((bq, bk, u, v, gamma, beta)):
                a1 = a.rearrange("h d -> (h d)") if len(a.shape) == 2 else a
                sp.dma_start(rows[r:r + 1, :], a1.rearrange("(a d) -> a d", a=1)).then_inc(s["c_in"], 16)
            sp.dma_start(rows[6:7, :], bq.rearrange("(a d) -> a d", a=1)).then_inc(s["c_in"], 16)
            for dst, a in ((wq_sb, Wq), (wk_sb, Wk), (wv_sb, Wv), (wp_sb, Wpos), (wf_sb[:, :], Wf), (wr_f, Wr),
                           (pe_sb, peT), (idf[:, :], ident), (selb[:, :, :, :, :], sel)):
                sp.dma_start(dst, a).then_inc(s["c_in"], 16)
            sp.dma_start(bv_bc, bv.partition_broadcast(P)).then_inc(s["c_in"], 16)
            sp.dma_start(bf_bc, bf.partition_broadcast(P)).then_inc(s["c_in"], 16)
            sp.dma_start(tri_sb.rearrange("p e j -> p (e j)"), tri.partition_broadcast(P)).then_inc(s["mask"], 16)
            for e in range(E):
                r = e % 2
                ge(sp, "w2_lo", e - 1)
                sp.dma_start(wstage[:, r, :], W13[e]).then_inc(s_w[r], 16)
                sp.dma_start(w2stage[:, r, 0:FT - 1, :],
                             W2[e, 0:(FT - 1) * P, :].rearrange("(f p) d -> p f d", p=P)).then_inc(s_w[r], 16)
                sp.dma_start(w2stage[0:FW[-1], r, FT - 1, :], W2[e, (FT - 1) * P:F, :]).then_inc(s_w[r], 16)

            def write_scores(n, g):
                ge(sp, "bdev", U * n + T * (g + 1))
                met(sp)
                if not isinstance(n, int) or n > 0:
                    ge(sp, s_bdr[g], 16 * n)
                    met(sp)
                sp.dma_start(scratch[g].rearrange("(p w) -> p w", p=P),
                             bdw[:, g % 2, :, :].rearrange("p t s -> p (t s)")).then_inc(s_bdw[g % 2], 16)

            def read_scores(n, g):
                ge(sp, s_bdw[g % 2], 16 * (2 * n + g // 2 + 1))
                met(sp)
                ge(sp, "t", U * (n - 1) + T * (g + 1))
                met(sp)
                sp.dma_start(bdr[:, g, :, :].rearrange("p t s -> p (t s)"),
                             scratch[g, S:S * (S + 1)].rearrange("(p w) -> p w", p=P)).then_inc(s_bdr[g], 16)

            ge(sp, "w2_lo", E)
            for g in range(GH):
                write_scores(0, g)
            ge(sp, "cwd", 1)
            for g in range(RA):
                read_scores(0, g)

            def body(n, last):
                for g in range(GH):
                    if g + RA < GH:
                        read_scores(n, g + RA)
                    elif not last:
                        read_scores(n + 1, g + RA - GH)
                    if not last:
                        write_scores(n + 1, g)

            body(0, False)
            with sp.Fori(1, N - 1) as n:
                body(n, False)
            body(N - 1, True)

            with sp.Fori(0, B) as b:
                sp.wait_ge(s["fo"], b + 1)
                met(sp)
                sp.dma_start(out[ds(b, 1)].rearrange("a (p t) d -> p (a t d)", t=T),
                             acc[:, ds(b, 1), :, :].rearrange("p a t d -> p (a t d)")).then_inc(s_out, 16)
            sp.wait_ge(s_out, 16 * B)

        @block.gpsimd
        def _(pool):
            for e in range(E):
                r = e % 2
                pool.wait_ge(s_w[r], 48 * (e // 2 + 1))
                pool.tensor_copy(w13[:, 0, e, :], wstage[:, r, :]).then_inc(s["w13_hi"], 1)
                pool.tensor_copy(w2[:, 0, e, 0:FT - 1, :], w2stage[:, r, 0:FT - 1, :]).then_inc(s["w2_hi"], 1)
                pool.tensor_copy(w2[0:FW[-1], 0, e, FT - 1, :], w2stage[0:FW[-1], r, FT - 1, :]).then_inc(s["w2_hi"], 1)
                pool.wait_ge(s["w13_hi"], e + 1)
                pool.tensor_tensor(w13[:, 1, e, :], wstage[:, r, :], w13[:, 0, e, :], ALU.subtract).then_inc(s["w13_lo"], 1)
                pool.wait_ge(s["w2_hi"], 2 * e + 2)
                pool.tensor_tensor(w2[:, 1, e, 0:FT - 1, :], w2stage[:, r, 0:FT - 1, :], w2[:, 0, e, 0:FT - 1, :],
                                   ALU.subtract)
                pool.wait_ge(s["w13_lo"], e + 1)
                pool.tensor_tensor(w2[0:FW[-1], 1, e, FT - 1, :], w2stage[0:FW[-1], r, FT - 1, :],
                                   w2[0:FW[-1], 0, e, FT - 1, :], ALU.subtract).then_inc(s["w2_lo"], 1)
            for b in range(B):
                pool.wait_ge(s["nrm1"], b + 1)
                pool.tensor_tensor(acc[:, b, :, :], acc[:, b, :, :],
                                   bf_bc.unsqueeze(1).broadcast_to([P, T, D]), ALU.add).then_inc(s["accd"], 1)
            pool.wait_ge(s["cwd"], 1)
            pool.memset(bdw[:, :, :, 0:1], 0.0).then_inc(s["zc"], 1)

            def split_hidden(n, su, f):
                j = NU * FT * n + FT * su + f
                w = FW[f]
                ge(pool, "h_d", j + 1)
                ge(pool, "y", T * (NU * n + su))
                met(pool)
                pool.tensor_copy(hh[0:w, f, :], hb[0:w, j_ring(su, f), :]).then_inc(s["hhi"], 1)
                ge(pool, "hhi", j + 1)
                pool.tensor_tensor(hl[0:w, f, :], hb[0:w, j_ring(su, f), :], hh[0:w, f, :], ALU.subtract).then_inc(s["hlo"], 1)

            def norm_heads(n):
                ge(pool, "oc", n + 1)
                o = ob[:, :].rearrange("p (i k d) -> p i k d", k=2, d=HD)
                pool.tensor_tensor(tmp[:, :, :], o[:, :, 0, :], o[:, :, 1, :], ALU.add).then_inc(s["ou"], 1)
                ge(pool, "ou", n + 1)
                out_n = heads[:, ds(n, 1), :].rearrange("p a m -> p (a m)").rearrange("p (i d) -> p i d", d=HD)
                pool.tensor_tensor(out_n, tmp[:, :, :], rs[:, :].unsqueeze(2).broadcast_to([P, U, HD]),
                                   ALU.mult).then_inc(s["oev"], 1)

            def body(n, first):
                for i in range(U):
                    if i in HIDDEN_AT:
                        split_hidden(n, *HIDDEN_AT[i])
                    if i == LV and not first:
                        norm_heads(n - 1)

            body(0, True)
            with pool.Fori(1, N) as n:
                body(n, False)
            norm_heads(N - 1)

            def gather_heads(b, r):
                pool.wait_ge(s["oev"], N)
                ge(pool, "fT", b - r)
                met(pool)
                dst = (Pb_f if r else Sb_f)[:, 0:T * D].rearrange("p (t n m) -> p n t m", t=T, n=NG)
                for n in range(NG):
                    src = heads[:, ds(b * NG + n, 1), :].rearrange("p a m -> p (a m)")
                    ins = pool.tensor_copy(dst[:, n].rearrange("p t (g d) -> p t g d", d=HD),
                                           src.rearrange("p (g t d) -> p t g d", g=GH, t=T))
                ins.then_inc(s["gath"], 1)

            gather_heads(0, 0)
            gather_heads(1, 1)
            with pool.Fori(1, B // 2) as i:
                for r in range(2):
                    gather_heads(2 * i + r, r)

        @block.scalar
        def _(act):
            act.wait_ge(s["rowsT"], 1)
            act.activation(cols[:, 0:6], misc[:, 0:6], ACT.Copy).then_inc(s["cols_c"], 1)
            act.wait_ge(s["p_mm"], 1)
            act.activation(pT_h, bank[2][:, :], ACT.Copy).then_inc(s["p_hi"], 1)
            for g in range(NG):
                act.wait_ge(s["p_rep"], g + 1)
                act.activation(pall[:, g, :], bank[3 + g % 2][:, :], ACT.Copy).then_inc(s["p_all"], 1)
            act.wait_ge(s["cols_s"], 2)
            def batch(b, r):
                act.wait_ge(s["ve"], b + 1)
                act.activation(sd1, sd1, ACT.Sqrt).then_inc(s["sd"], 1)
                act.wait_ge(s["ve2"], b + 1)
                act.activation(sd2, sd2, ACT.Sqrt).then_inc(s["sd2"], 1)
                act.wait_ge(s["x1T"], b + 1)
                act.activation(xnT[:, 0, ds(b, 1), :].rearrange("p a s -> p (a s)"), bank[0][:, :],
                               ACT.Copy).then_inc(s["xhi"], 1)
                act.wait_ge(s["x2Tm"], b + 1)
                act.activation(x2T[:, r, :].rearrange("p (q t) -> p q t", t=T),
                               bank[1][:, :].rearrange("p (t q) -> p q t", t=T),
                               ACT.Identity, bias=cols[:, 5:6], scale=cols[:, 4:5]).then_inc(s["x2Tc"], 1)
                act.wait_ge(s["qkv"], 3 * b + 1)
                act.activation(quT[:, 0, ds(b, 1), :].rearrange("p a s -> p (a s)"), bank[3][:, :], ACT.Identity,
                               bias=cols[:, 6:7]).then_inc(s["qu_hi"], 1)
                act.activation(qvT[:, 0, ds(b, 1), :].rearrange("p a s -> p (a s)"), bank[3][:, :], ACT.Identity,
                               bias=cols[:, 7:8]).then_inc(s["qv_hi"], 1)
                act.wait_ge(s["qkv"], 3 * b + 2)
                act.activation(kT[:, 0, ds(b, 1), :].rearrange("p a s -> p (a s)"), bank[4][:, :], ACT.Identity,
                               bias=cols[:, 1:2]).then_inc(s["k_hi"], 1)
                for c in range(T):
                    act.wait_ge(s["v_c"], b + 1)
                    ins = act.activation(v_part(b, c, 0), v_rows(c), ACT.Copy)
                ins.then_inc(s["v_hi"], 1)

            batch(0, 0)
            batch(1, 1)
            with act.Fori(1, B // 2) as i:
                for r in range(2):
                    batch(2 * i + r, r)
            act.wait_ge(s["route"], 1)
            act.activation(lg, lg, ACT.Exp).then_inc(s["ex"], 1)

            def evac_qv(n):
                ge(act, "qrep", n + 1)
                act.activation(qvs[:, :].rearrange("p (t q) -> p t q", t=T),
                               bd_ps[:, :].rearrange("p (q t) -> p t q", t=T), ACT.Copy).then_inc(s["qvs_r"], 1)

            def evac_k(n):
                ge(act, "krep", n + 1)
                act.activation(ks[:, :], x3_ps[:, :], ACT.Copy).then_inc(s["ks_r"], 1)

            def evac_scores(n, i):
                g, t = divmod(i, T)
                if t == 0:
                    ge(act, s_bdw[g % 2], 16 * (2 * n + g // 2))
                ge(act, "bd", U * n + i + 1)
                act.activation(bdw[:, g % 2, t, 1:S + 1], bd_ps[:, :], ACT.Copy).then_inc(s["bdev"], 1)

            def softmax_exp(n, i):
                k = U * n + i
                ge(act, "ttr", k + 1)
                e = bdr[:, i // T, i % T, :]
                act.activation(e, e, ACT.Exp, bias=nmax[:, i:i + 1], scale=-1.0,
                               accum_out=sums[:, ds(n % 2, 1), i:i + 1].rearrange("p a b -> p (a b)")).then_inc(s["ex_d"], 1)

            def evac_hi(n, i):
                k = U * n + i
                ge(act, "t", k + 1)
                ge(act, "pv", k - 1)
                act.activation(PTh[:, i % 2, :], tp_ps[i % 2][:, :], ACT.Copy).then_inc(s["thi"], 1)

            def gate(n, su, f):
                j = NU * FT * n + FT * su + f
                w = FW[f]
                ge(act, "x13", j + 1)
                ge(act, "hlo", j - 1)
                act.activation(hb[0:w, j_ring(su, f), :], x1_ps[0:w, :], ACT.Tanh, scale=0.5).then_inc(s["thd"], 1)

            def body(n, first, last, ahead=True):
                for i in range(U):
                    if not last:
                        evac_scores(n + 1, i)
                    if i == U - 1 and not last:
                        evac_k(n + 1)
                        if ahead:
                            evac_qv(n + 2)
                    if i - 1 in HIDDEN_AT:
                        gate(n, *HIDDEN_AT[i - 1])
                    softmax_exp(n, i)
                    if i >= LT:
                        evac_hi(n, i - LT)
                    elif not first:
                        evac_hi(n - 1, U + i - LT)

            act.wait_ge(s["zc"], 1)
            evac_qv(0)
            for i in range(U):
                evac_scores(0, i)
            evac_k(0)
            evac_qv(1)
            body(0, True, False)
            with act.Fori(1, N - 2) as n:
                body(n, False, False)
            body(N - 2, False, False, ahead=False)
            body(N - 1, False, True)
            for i in range(U - LT, U):
                evac_hi(N - 1, i)
            def evac_heads(b, r):
                ge(act, "fT", b + 1)
                ge(act, "fy", b - r)
                act.activation(aT[:, r, :], bank[0][:, :], ACT.Copy).then_inc(s["fTc"], 1)

            evac_heads(0, 0)
            evac_heads(1, 1)
            with act.Fori(1, B // 2) as i:
                for r in range(2):
                    evac_heads(2 * i + r, r)

        @block.tensor
        def _(pe):
            pe.wait_ge(s["c_in"], 16 * 18)
            pe.transpose(misc[:, 0:7], rows, idf[0:7, 0:7]).then_inc(s["rowsT"], 1)
            pe.matmul(bank[2][:, :], wp_sb, pe_sb, start=True, stop=True).then_inc(s["p_mm"], 1)
            pe.wait_ge(s["p_hi"], 1)
            pe.wait_ge(s["p_lo"], 1)
            for g in range(NG):
                ge(pe, "p_all", g - 1)
                for part, src in enumerate((pT_h, pT_l)):
                    mm = pe.matmul(bank[3 + g % 2][:, :], selb[:, 1, part, g, :], src, start=(part == 0), stop=(part == 1))
                mm.then_inc(s["p_rep"], 1)
            pe.wait_ge(s["p_all"], NG)
            pe.wait_ge(s["wr_lo"], 1)
            def batch(b, r):
                pe.wait_ge(s["nrm1"], b + 1)
                ge(pe, "xlo", b)
                for t in range(T):
                    mm = pe.transpose(bank[0][:, t * P:(t + 1) * P], xn1[:, r, t, :],
                                      idf[:, :])
                mm.then_inc(s["x1T"], 1)
                pe.wait_ge(s["nrm2"], b + 1)
                ge(pe, "x2Tc", b)
                for t in range(T):
                    mm = pe.transpose(bank[1][:, t * P:(t + 1) * P], xn2[:, r, t, :],
                                      idf[:, :])
                mm.then_inc(s["x2Tm"], 1)
                pe.wait_ge(s["x2Tc"], b + 1)
                xt = x2T[:, r, :]
                ge(pe, "qv_lo", b)
                pe.matmul(bank[3][:, :], wq_sb, xt, start=True, stop=True).then_inc(s["qkv"], 1)
                ge(pe, "k_lo", b)
                pe.matmul(bank[4][:, :], wk_sb, xt, start=True, stop=True).then_inc(s["qkv"], 1)
                ge(pe, "v_c", b)
                for c in range(T):
                    mm = pe.matmul(bank[5][:, c * D:(c + 1) * D],
                                   x2T[:, r, c * P:(c + 1) * P], wv_sb, start=True, stop=True)
                mm.then_inc(s["qkv"], 1)
                pe.wait_ge(s["xlo"], b + 1)
                terms = hi_lo_terms(4)
                for t in range(T):
                    for m, (a, w) in enumerate(terms):
                        mm = pe.matmul(misc[:, ds((b * T + t) * E, E)],
                                       xnT[:, a, ds(b, 1), t * P:(t + 1) * P].rearrange("p a s -> p (a s)"),
                                       wr_l if w else wr_h, start=(m == 0), stop=(m == 3))
                mm.then_inc(s["lgm"], 1)

            batch(0, 0)
            batch(1, 1)
            with pe.Fori(1, B // 2) as i:
                for r in range(2):
                    batch(2 * i + r, r)
            pe.wait_ge(s["lgc"], 1)
            pe.wait_ge(s["v_lo"], B)
            pe.wait_ge(s["k_lo"], B)
            pe.wait_ge(s["qv_lo"], B)
            pe.wait_ge(s["w2_lo"], E)

            def replicate(dst, src, pattern, n):
                for part in range(2):
                    mm = pe.matmul(dst[:, :], selb[:, pattern, part, ds(n % NG, 1), :].rearrange("p a m -> p (a m)"),
                                   src[:, part, ds(n // NG, 1), :].rearrange("p a s -> p (a s)"),
                                   start=(part == 0), stop=(part == 1))
                return mm

            def rep_qv(n):
                if not isinstance(n, int) or n > 0:
                    ge(pe, "bdev", U * n)
                replicate(bd_ps, qvT, 0, n).then_inc(s["qrep"], 1)

            def rep_qu_k(n):
                if not isinstance(n, int) or n > 0:
                    ge(pe, "h_d", NU * FT * n)
                replicate(x1_ps, quT, 0, n).then_inc(s["vrep"], 1)
                replicate(x3_ps, kT, 1, n).then_inc(s["krep"], 1)

            def position_scores(n, i):
                g, t = divmod(i, T)
                if i == 0:
                    ge(pe, "qvs_r", n + 1)
                    ge(pe, "ps_r", n + 1)
                ge(pe, "bdev", U * n + i)
                r = slice(SLOT * g, SLOT * (g + 1))
                pe.matmul(bd_ps[:, :], qvs[r, t * P:(t + 1) * P], ps[r, :], start=True, stop=True).then_inc(s["bd"], 1)

            def content_scores(n, i):
                g, t = divmod(i, T)
                if i == 0:
                    ge(pe, "qus_r", n + 1)
                    ge(pe, "ks_r", n + 1)
                ge(pe, "ttr", U * n + i)
                r = slice(SLOT * g, SLOT * (g + 1))
                pe.matmul(ac_ps[:, :], qus[r, t * P:(t + 1) * P], ks[r, :], start=True, stop=True).then_inc(s["ac"], 1)

            def transposes(n, i):
                k = U * n + i
                ge(pe, "ex_d", k + 1)
                ge(pe, "te", k - 1)
                for c in range(T):
                    mm = pe.transpose(tp_ps[i % 2][:, c * P:(c + 1) * P], bdr[:, i // T, i % T, c * P:(c + 1) * P], idf[:, :])
                mm.then_inc(s["t"], 1)

            def weighted_v(n, i):
                g, t = divmod(i, T)
                k = U * n + i
                ge(pe, "te", k + 1)
                if i == 0:
                    ge(pe, "oc", n)
                steps = [(c, pt) for c in range(T) for pt in (PTh, PTl)]
                for m, (c, pt) in enumerate(steps):
                    mm = pe.matmul(misc[:, i * 2 * HD:(i + 1) * 2 * HD], pt[:, i % 2, c * P:(c + 1) * P],
                                   vv[:, ds(n, 1), c, g, :, :].rearrange("p a k d -> p (a k d)"),
                                   start=(m == 0), stop=(m == len(steps) - 1))
                mm.then_inc(s["pv"], 1)

            def hidden(n, su, f):
                j = NU * FT * n + FT * su + f
                w = FW[f]
                ge(pe, "h_d", j)
                e, b = n // NG, NU * (n % NG) + su
                for dst, o in ((x1_ps, 0), (x3_ps, F)):
                    for m, (wp, xp) in enumerate(hi_lo_terms(3)):
                        mm = pe.matmul(dst[0:w, :],
                                       w13[:, wp, ds(e, 1), o + P * f:o + P * f + w].rearrange("p a m -> p (a m)"),
                                       xnT[:, xp, ds(b, 1), :].rearrange("p a s -> p (a s)"),
                                       start=(m == 0), stop=(m == 2))
                mm.then_inc(s["x13"], 1)

            def down(n, su, t):
                y = T * (NU * n + su) + t
                e = n // NG
                if t == 0:
                    ge(pe, "hlo", FT * (NU * n + su) + FT)
                    ge(pe, "accs", T * (NU * n + su))
                o = t * D
                steps = [(f, hp, wp) for f in range(FT) for hp, wp in hi_lo_terms(3)]
                for m, (f, hp, wp) in enumerate(steps):
                    w = FW[f]
                    h = (hl if hp else hh)[0:w, f, t * P:(t + 1) * P]
                    mm = pe.matmul(y_ps[:, o:o + D], h, w2[0:w, wp, ds(e, 1), f, :].rearrange("p a d -> p (a d)"),
                                   start=(m == 0), stop=(m == len(steps) - 1))
                mm.then_inc(s["y"], 1)

            def body(n, first, last, ahead=True):
                for i in range(U):
                    content_scores(n, i)
                    if not last:
                        position_scores(n + 1, i)
                    if i == U - 1 and not last:
                        rep_qu_k(n + 1)
                        if ahead:
                            rep_qv(n + 2)
                    if i >= LV:
                        weighted_v(n, i - LV)
                    elif not first:
                        weighted_v(n - 1, U + i - LV)
                    if i >= LT:
                        transposes(n, i - LT)
                    elif not first:
                        transposes(n - 1, U + i - LT)
                    if i in HIDDEN_AT:
                        hidden(n, *HIDDEN_AT[i])
                    su, tiles = DOWN_AT.get(i, (0, ()))
                    for t in tiles:
                        if not (su and first):
                            down(n - su, su, t)

            rep_qv(0)
            for i in range(U):
                position_scores(0, i)
            rep_qu_k(0)
            rep_qv(1)
            body(0, True, False)
            with pe.Fori(1, N - 2) as n:
                body(n, False, False)
            body(N - 2, False, False, ahead=False)
            body(N - 1, False, True)
            for i in range(U, U + LV):
                weighted_v(N - 1, i - LV)
                if i - LT < U:
                    transposes(N - 1, i - LT)

            for t in range(T):
                down(N - 1, 1, t)

            pe.wait_ge(s["oev"], N)
            pe.wait_ge(s["accs"], N * NU * T)
            def project(b, r):
                pe.wait_ge(s["gath"], b + 1)
                ge(pe, "fTc", b)
                for t in range(T):
                    mm = pe.transpose(bank[0][:, t * P:(t + 1) * P], Sb_f[:, t * D:(t + 1) * D] if r == 0 else
                                      Pb_f[:, t * D:(t + 1) * D], idf[:, :])
                mm.then_inc(s["fT"], 1)
                pe.wait_ge(s["fTc"], b + 1)
                ge(pe, "fo", b)
                for t in range(T):
                    mm = pe.matmul(bank[2][:, t * D:(t + 1) * D], aT[:, r, t * P:(t + 1) * P], wf_sb[:, :],
                                   start=True, stop=True)
                mm.then_inc(s["fy"], 1)

            project(0, 0)
            project(1, 1)
            with pe.Fori(1, B // 2) as i:
                for r in range(2):
                    project(2 * i + r, r)


        @block.vector
        def _(dve):
            V = nc.vector
            dve.wait_ge(s["cols_c"], 1)
            V.tensor_tensor(cols[:, 6:7], cols[:, 0:1], cols[:, 2:3], ALU.add).then_inc(s["cols_s"], 1)
            V.tensor_tensor(cols[:, 7:8], cols[:, 0:1], cols[:, 3:4], ALU.add).then_inc(s["cols_s"], 1)
            V.tensor_copy(wr_h, wr_f).then_inc(s["wr_hi"], 1)
            dve.wait_ge(s["wr_hi"], 1)
            V.tensor_tensor(wr_l, wr_f, wr_h, ALU.subtract).then_inc(s["wr_lo"], 1)
            dve.wait_ge(s["p_hi"], 1)
            V.tensor_tensor(pT_l, bank[2][:, :], pT_h, ALU.subtract).then_inc(s["p_lo"], 1)
            dve.wait_ge(s["cols_s"], 2)
            dve.wait_ge(s["x_in"], 16)

            def norm_rows(b, src, dst, mv, sd, rd, s_st, s_ag, s_ve, s_sd, s_rd, s_nrm):
                ge(dve, s_ag, T * b)
                for t in range(T):
                    V.bn_stats(st6[:, t, :], src(t)).then_inc(s[s_st], 1)
                for t in range(T):
                    dve.wait_ge(s[s_st], T * b + t + 1)
                    met(dve)
                    V.bn_aggr(mv[:, t, :], st6[:, t, :]).then_inc(s[s_ag], 1)
                dve.wait_ge(s[s_ag], T * (b + 1))
                V.tensor_scalar(sd, mv[:, :, 1], EPS, None, ALU.add).then_inc(s[s_ve], 1)
                dve.wait_ge(s[s_sd], b + 1)
                V.reciprocal(rd, sd).then_inc(s[s_rd], 1)
                dve.wait_ge(s[s_rd], b + 1)
                for t in range(T):
                    ins = V.tensor_scalar(dst(t), src(t), mv[:, t, 0:1], rd[:, t:t + 1], ALU.subtract, ALU.mult)
                ins.then_inc(s[s_nrm], 1)

            def batch(b, ring):
                def tile_of(a, r):
                    return lambda t: a[:, r, t, :] if isinstance(r, int) else \
                        a[:, ds(r, 1), t, :].rearrange("p a d -> p (a d)")
                norm_rows(b, tile_of(acc, b), tile_of(xn1, ring), mv1, sd1, rd1, "st", "ag", "ve", "sd", "rd", "nrm1")
                dve.wait_ge(s["nrm1"], b + 1)
                norm_rows(b, tile_of(xn1, ring), tile_of(xn2, ring), mv2, sd2, rd2, "st2", "ag2", "ve2", "sd2", "rd2",
                          "nrm2")

                def low(name, dst, src, hi, bias, after, count):
                    dve.wait_ge(s[after], count)
                    one = lambda a: a[:, ds(b, 1), :].rearrange("p a s -> p (a s)")
                    if bias is None:
                        V.tensor_tensor(one(dst), src, one(hi), ALU.subtract).then_inc(s[name], 1)
                    else:
                        V.scalar_tensor_tensor(out=one(dst), in0=src, scalar=bias, in1=one(hi), op0=ALU.add,
                                               op1=ALU.subtract).then_inc(s[name], 1)

                low("xlo", xnT[:, 1], bank[0][:, :], xnT[:, 0], None, "xhi", b + 1)
                low("qu_lo", quT[:, 1], bank[3][:, :], quT[:, 0], cols[:, 6:7], "qv_hi", b + 1)
                low("qv_lo", qvT[:, 1], bank[3][:, :], qvT[:, 0], cols[:, 7:8], "qv_hi", b + 1)
                low("k_lo", kT[:, 1], bank[4][:, :], kT[:, 0], cols[:, 1:2], "k_hi", b + 1)
                dve.wait_ge(s["qkv"], 3 * b + 3)
                ge(dve, "v_lo", b)
                V.tensor_tensor(hb[:, 0, :].rearrange("p (c d) -> p c d", c=T),
                                bank[5][:, :].rearrange("p (c d) -> p c d", c=T),
                                bv_bc.unsqueeze(1).broadcast_to([P, T, D]), ALU.add).then_inc(s["v_c"], 1)
                dve.wait_ge(s["v_hi"], b + 1)
                for c in range(T):
                    ins = V.tensor_tensor(v_part(b, c, 1), v_rows(c), v_part(b, c, 0), ALU.subtract)
                ins.then_inc(s["v_lo"], 1)

            batch(0, 0)
            batch(1, 1)
            with dve.Fori(1, B // 2) as i:
                for r in range(2):
                    batch(2 * i + r, r)

            chain = [0]

            def step(ins):
                ins.then_inc(s["selq"], 1)
                chain[0] += 1
                dve.wait_ge(s["selq"], chain[0])

            dve.wait_ge(s["lgm"], B)
            dve.wait_ge(s["mask"], 16)
            V.tensor_copy(lg, misc[:, 0:BT * E].rearrange("p (i e) -> p i e", e=E)).then_inc(s["lgc"], 1)
            dve.wait_ge(s["lgc"], 1)
            step(V.tensor_reduce(mx, lg, AX.X, ALU.max))
            V.tensor_tensor(lg, lg, mx.unsqueeze(2).broadcast_to([P, BT, E]), ALU.subtract).then_inc(s["route"], 1)
            dve.wait_ge(s["ex"], 1)
            dve.wait_ge(s["w2_lo"], E)
            pj = lg.unsqueeze(2).broadcast_to([P, BT, E, E])
            pi = lg.unsqueeze(3).broadcast_to([P, BT, E, E])
            step(V.tensor_tensor(cmp1, pj, pi, ALU.is_gt))
            step(V.tensor_tensor(cmp2, pj, pi, ALU.is_equal))
            step(V.tensor_tensor(cmp2, cmp2, tri_sb.unsqueeze(1).broadcast_to([P, BT, E, E]), ALU.mult))
            step(V.tensor_tensor(cmp1, cmp1, cmp2, ALU.add))
            step(V.tensor_reduce(rank, cmp1, AX.X, ALU.add))
            step(V.tensor_scalar(rank, rank, float(TOPK), 0.5, ALU.is_lt, ALU.mult))
            step(V.tensor_tensor(rank, rank, lg, ALU.mult))
            step(V.tensor_reduce(den, rank, AX.X, ALU.add))
            step(V.tensor_scalar(den, den, 2.0, None, ALU.mult))
            step(V.reciprocal(rden, den))
            V.tensor_tensor(cw[:, :, :], rank, rden.unsqueeze(2).broadcast_to([P, BT, E]), ALU.mult).then_inc(s["cwd"], 1)
            dve.wait_ge(s["accd"], B)
            dve.wait_ge(s["cwd"], 1)

            def evac_qu(n):
                ge(dve, "vrep", n + 1)
                V.tensor_copy(qus[:, :].rearrange("p (t q) -> p t q", t=T),
                              x1_ps[:, :].rearrange("p (q t) -> p t q", t=T)).then_inc(s["qus_r"], 1)

            def add_scores(n, i):
                g, t = divmod(i, T)
                k = U * n + i
                ge(dve, "ac", k + 1)
                if t == 0:
                    ge(dve, s_bdr[g], 16 * (n + 1))
                ge(dve, "ex_d", k - U + 1) if not isinstance(n, int) or n > 0 else None
                met(dve)
                V.tensor_tensor_reduce(out=bdr[:, g, t, :], in0=ac_ps[:, :], in1=bdr[:, g, t, :],
                                       scale=-SCALE, scalar=3.0e38, op0=ALU.add, op1=ALU.min,
                                       accum_out=nmax[:, i:i + 1]).then_inc(s["ttr"], 1)

            def evac_T(n, i):
                k = U * n + i
                ge(dve, "thi", k + 1)
                ge(dve, "pv", k - 1)
                V.tensor_tensor(PTl[:, i % 2, :], tp_ps[i % 2][:, :], PTh[:, i % 2, :], ALU.subtract).then_inc(s["te"], 1)

            def evac_out(n):
                ge(dve, "pv", U * (n + 1))
                ge(dve, "oev", n)
                V.tensor_copy(ob[:, :], misc[:, 0:U * 2 * HD])
                V.reciprocal(rs[:, :], sums[:, ds(n % 2, 1), :].rearrange("p a i -> p (a i)")).then_inc(s["oc"], 1)

            def copy_p(n):
                ge(dve, "p_all", NG)
                if not isinstance(n, int) or n > 0:
                    ge(dve, "bd", U * n)
                V.tensor_copy(ps[:, :], pall[:, ds(n % NG, 1), :].rearrange("p a s -> p (a s)")).then_inc(s["ps_r"], 1)

            def hidden(n, su, f):
                j = NU * FT * n + FT * su + f
                w = FW[f]
                ge(dve, "thd", j + 1)
                h = hb[0:w, j_ring(su, f), :]
                V.scalar_tensor_tensor(out=h, in0=h, scalar=1.0, in1=x1_ps[0:w, :], op0=ALU.add,
                                       op1=ALU.mult).then_inc(s["a_d"], 1)
                ge(dve, "a_d", j + 1)
                V.tensor_tensor(h, h, x3_ps[0:w, :], ALU.mult).then_inc(s["h_d"], 1)

            def add_expert(n, su, t):
                y = T * (NU * n + su) + t
                e, b = n // NG, NU * (n % NG) + su
                ge(dve, "y", T * (NU * n + su + 1))
                ge(dve, "accs", T * (NU * n + su))
                a = acc[:, ds(b, 1), t, :].rearrange("p a d -> p (a d)")
                V.scalar_tensor_tensor(out=a, in0=y_ps[:, t * D:(t + 1) * D],
                                       scalar=cw[:, ds(b * T + t, 1), ds(e, 1)].rearrange("p a e -> p (a e)"),
                                       in1=a, op0=ALU.mult, op1=ALU.add).then_inc(s["accs"], 1)

            def add_experts(n, i, first):
                su, tiles = DOWN_AT.get(i, (0, ()))
                if T - 1 in tiles and not (su and first):
                    for t in range(T):
                        add_expert(n - su, su, t)

            def body(n, first, last, ahead=True):
                for i in range(U + 1):
                    if i < U:
                        if i == LV and not first:
                            evac_out(n - 1)
                        add_scores(n, i)
                        if i == U - 1 and not last:
                            evac_qu(n + 1)
                            if ahead:
                                copy_p(n + 2)
                        if i >= LL:
                            evac_T(n, i - LL)
                        elif not first:
                            evac_T(n - 1, U + i - LL)
                    if i - 1 in HIDDEN_AT:
                        hidden(n, *HIDDEN_AT[i - 1])
                    add_experts(n, i - 1, first)

            copy_p(0)
            evac_qu(0)
            copy_p(1)
            body(0, True, False)
            with dve.Fori(1, N - 2) as n:
                body(n, False, False)
            body(N - 2, False, False, ahead=False)
            body(N - 1, False, True)
            for i in range(U - LL, U):
                evac_T(N - 1, i)
            evac_out(N - 1)
            for t in range(T):
                add_expert(N - 1, 1, t)

            with dve.Fori(0, B) as b:
                dve.wait_ge(s["fy"], b + 1)
                a = acc[:, ds(b, 1), :, :].rearrange("p a t d -> p (a t d)")
                V.tensor_tensor(a, a, bank[2][:, :], ALU.add).then_inc(s["fo"], 1)


_INS = ['L0_attn_x', 'L0_attn_Wq', 'L0_attn_bq', 'L0_attn_Wk', 'L0_attn_bk', 'L0_attn_Wv', 'L0_attn_bv',
        'L0_attn_Wpos', 'L0_attn_Wf', 'L0_attn_bf', 'L0_attn_u', 'L0_attn_v', 'L0_attn_gamma', 'L0_attn_beta',
        'L0_ffn_W13', 'L0_ffn_W2', 'L0_ffn_Wr']


def shape_constants(S, D, H, HD, E):
    import numpy as np

    pos = np.arange(S, dtype=np.float32)
    inv_freq = (np.float32(1.0) / np.power(np.float32(10000.0), np.arange(0.0, D, 2.0, dtype=np.float32) / np.float32(D)))
    angles = pos[:, None] * inv_freq[None, :].astype(np.float32)
    pe = np.zeros((S, D), np.float32)
    pe[:, 0::2] = np.sin(angles)
    pe[:, 1::2] = np.cos(angles)
    sel = np.zeros((H, HD, 2, 2, H // 4, 4, 4, HD), np.float16)
    for h in range(H):
        for d in range(HD):
            for pattern, parts in enumerate(((0, 0, 1, 1), (0, 1, 0, 1))):
                for copy, part in enumerate(parts):
                    sel[h, d, pattern, part, h // 4, h % 4, copy, d] = 1.0
    tri = np.tril(np.ones((E, E), np.float32), -1)
    return {
        "peT": np.ascontiguousarray(pe.T), "ident": np.eye(128, dtype=np.float32),
        "sel": sel.reshape(H * HD, 2, 2, H // 4, 128), "tri": tri.reshape(-1),
    }


def kernel(**inputs):
    import numpy as _np
    import concourse.bacc as _bacc
    from concourse import mybir as _mybir
    from concourse.bass_utils import run_bass_kernel_spmd as _run

    nc = _bacc.Bacc("TRN2", target_bir_lowering=False, num_devices=1)
    arrays, args = {}, []
    given = {n: _np.ascontiguousarray(inputs[n]) for n in _INS}
    B, S, D = given['L0_attn_x'].shape
    H, HD = given['L0_attn_u'].shape
    E = given['L0_ffn_Wr'].shape[1]
    given.update(shape_constants(S, D, H, HD, E))
    for name, a in given.items():
        arrays[f"in_{name}_dram"] = a
        args.append(nc.dram_tensor(f"in_{name}_dram", a.shape, _mybir.dt.from_np(a.dtype), kind="ExternalInput").ap())
    args.append(nc.dram_tensor("out_0_dram", (B, S, D), F32, kind="ExternalOutput").ap())
    build(nc, *args)
    r = _run(nc, [arrays], core_ids=[0])
    return r.results[0]["out_0_dram"]
```

```python
from contextlib import ExitStack

import concourse.bass as bass
from concourse import mybir

ALU = mybir.AluOpType
ACT = mybir.ActivationFunctionType
AX = mybir.AxisListType
F32 = mybir.dt.float32
F16 = mybir.dt.float16
ds = bass.ds

P = 128
EPS = 1e-5
TOPK = 2


def build(nc, x, Wq, bq, Wk, bk, Wv, bv, Wpos, Wf, bf, u, v, gamma, beta, W13, W2, Wr, peT, ident, sel, order, out):
    B, S, D = x.shape
    H, HD = u.shape
    E, F, _ = W2.shape
    T = S // P
    GH = 4
    NG = H // GH
    N = B * NG
    U = GH * T
    FT = -(-F // P)
    FW = [min(P, F - P * f) for f in range(FT)]
    NU = B * E // N
    SCALE = 1.0 / float(D) ** 0.5
    SLOT = P // GH
    assert D == P and S == T * P and SLOT == 4 * HD and NU == 2 and E == 8 and NG == 4

    GATE_AT = {0: (0, 0), 2: (0, 1), 6: (0, 2), 8: (1, 0), 10: (1, 1), 14: (1, 2)}
    LINEAR_AT = {1: (0, 0), 5: (0, 1), 7: (0, 2), 9: (1, 0), 13: (1, 1), 15: (1, 2)}
    DOWN_AT = {3: (1, (0, 1)), 4: (1, (2, 3)), 11: (0, (0, 1)), 12: (0, (2, 3))}

    with ExitStack() as ctx:
        def sb(name, shape, dt=F32):
            return ctx.enter_context(nc.sbuf_tensor(name, shape, dt))

        def sem(name):
            return ctx.enter_context(nc.semaphore(name))

        scratch = nc.dram_tensor("scratch", [GH, S * (S + 1)], F32).ap()
        records = nc.dram_tensor("records", [GH + B * H, SLOT, 3, S], F16).ap()

        acc = sb("acc", [P, B, T, D])
        xnT = sb("xnT", [P, 2, B, S], F16)
        quT = sb("quT", [P, 2, 2, S], F16)
        qvT = sb("qvT", [P, 2, 2, S], F16)
        kT = sb("kT", [P, 2, 2, S], F16)
        heads = sb("heads", [P, N, U * HD])
        vv = heads[:, :, :].bitcast(F16).rearrange("p n (c g k d) -> p n c g k d", c=T, g=GH, k=2)
        w13 = sb("w13", [P, 2, E, 2 * F], F16)
        w2 = sb("w2", [P, 2, E, FT, D], F16)
        pall = sb("pall", [P, NG, S], F16)
        idf = sb("idf", [P, P])
        selb = sb("selb", [P, 2, NG, P], F16)
        cw = sb("cw", [P, B * T, E])
        wf_sb = sb("wf_sb", [P, D])
        sums = sb("sums", [P, 2, U])
        rs = sb("rs", [P, U])
        turned = sb("turned", [P, D])
        nmax = sb("nmax", [P, U])
        bdr = sb("bdr", [P, GH, T, S])
        bdw = sb("bdw", [P, GH, T, S + 1])
        slots = sb("slots", [P, 3, S], F16)
        qus, ks, qvs = (slots[:, j, :] for j in range(3))
        ps = sb("ps", [P, S], F16)
        PTh = sb("PTh", [P, 2, S], F16)
        PTl = sb("PTl", [P, 2, S], F16)
        tmp = sb("tmp", [P, U, HD])
        ob = sb("ob", [P, U * 2 * HD])
        hb = sb("hb", [P, 2, S])
        hh = sb("hh", [P, 2, FT, S], F16)
        hl = sb("hl", [P, 2, FT, S], F16)
        stage = sb("stage", [P, 4 * F + 2 * FT * D])
        small = sb("small", [P, 2 * S])

        bank = [ctx.enter_context(nc.psum_tensor(f"bank{i}", [P, 512], F32)) for i in range(8)]
        ac_ps, y_ps, bd_ps, tp_ps, x1_ps, x3_ps, misc = bank[0], bank[1], bank[2], bank[3:5], bank[5], bank[6], bank[7]

        bdr_f = bdr[:, :, :, :].rearrange("p a t s -> p (a t s)")
        xn1 = bdr_f[:, 8 * S:10 * S].rearrange("p (r t d) -> p r t d", r=2, t=T)
        xn2 = bdr_f[:, 10 * S:12 * S].rearrange("p (r t d) -> p r t d", r=2, t=T)
        x2T = bdr_f[:, 12 * S:14 * S].rearrange("p (r s) -> p r s", r=2)
        wstage = stage[:, 0:2 * 2 * F].rearrange("p (r f) -> p r f", r=2)
        w2stage = stage[:, 4 * F:4 * F + 2 * FT * D].rearrange("p (r f d) -> p r f d", r=2, f=FT)
        Sb_f = bdr_f[:, 14 * S:16 * S]
        wq_sb, wk_sb, wv_sb, wp_sb = (Sb_f[:, i * D:(i + 1) * D] for i in range(4))
        pe_sb = Sb_f[:, 4 * D:4 * D + S]
        Pb_f = small[:, :]
        rows = Pb_f[0:6, 0:D]
        bv_bc = Pb_f[:, D:2 * D]
        bf_bc = Pb_f[:, 2 * D:3 * D]
        cols = Pb_f[:, 3 * D:3 * D + 8]
        wr_f = Pb_f[:, 3 * D + 8:3 * D + 8 + E]
        mv1 = Pb_f[:, 3 * D + 32:3 * D + 32 + 2 * T].rearrange("p (t k) -> p t k", k=2)
        mv2 = Pb_f[:, 3 * D + 48:3 * D + 48 + 2 * T].rearrange("p (t k) -> p t k", k=2)
        st6 = Pb_f[:, 3 * D + 64:3 * D + 64 + 6 * T].rearrange("p (t k) -> p t k", k=6)
        sd1 = Pb_f[:, 3 * D + 96:3 * D + 96 + T]
        sd2 = Pb_f[:, 3 * D + 104:3 * D + 104 + T]
        rd1 = Pb_f[:, 3 * D + 112:3 * D + 112 + T]
        rd2 = Pb_f[:, 3 * D + 120:3 * D + 120 + T]
        order_bc = Pb_f[:, 4 * D:4 * D + E]
        BT = B * T
        lg = Pb_f[:, 5 * D:5 * D + BT * E].rearrange("p (i e) -> p i e", e=E)
        wr_h = hh[:, 0, 0, 0:E]
        wr_l = hh[:, 0, 0, E:2 * E]
        pT_h, pT_l = PTh[:, 0, :], PTl[:, 0, :]
        mx = hb[:, 0, 0:BT]
        den = hb[:, 0, 64:64 + BT]
        rden = hb[:, 0, 128:128 + BT]
        rank = hb[:, 1, BT * E:2 * BT * E].rearrange("p (i e) -> p i e", e=E)
        at = [hb[:, 1, 0:BT * E].rearrange("p (i e) -> p i e", e=E),
              stage[:, 0:BT * E].rearrange("p (i e) -> p i e", e=E)]
        rest = stage[:, BT * E:2 * BT * E].rearrange("p (i e) -> p i e", e=E)
        last = bdr[:, 0, 0, :].rearrange("p (t d) -> p t d", t=T)
        lastT = bdr[:, 0, 1, :]

        def j_ring(su, f):
            return (FT * su + f) % 2

        def v_part(b, c, k):
            return vv[:, ds(b * NG, NG), c, :, k, :] if not isinstance(b, int) else vv[:, b * NG:(b + 1) * NG, c, :, k, :]

        def v_rows(c):
            return hb[:, 0, c * D:(c + 1) * D].rearrange("p (n g d) -> p n g d", n=NG, g=GH)

        GATHER_AT, TURN_AT, PROJECT_AT = 4, 7, 8
        RA = 3
        LT, LL, LV = 2, 3, 4

        names = """tile_turned turned_copied tile_projected tile_added v_hi v_lo probs_hi outs_copied outs_summed
            rows_loaded consts_loaded weights_loaded0 weights_loaded1 x_loaded w13_hi w13_lo w2_hi w2_lo
            rows_turned cols_copied cols_summed wr_hi wr_lo pos_keys_ready pos_keys_hi pos_keys_lo
            pos_slots_ready pos_slots_copied order_loaded stats1 moments1 variance1 root1 inverse_root1
            normed1 stats2 moments2 variance2 root2 inverse_root2 normed2 bias_added normed1_turned x_hi
            x_lo normed2_turned x2T_ready qkv_ready qu_hi qv_hi k_hi qu_lo qv_lo k_lo v_ready logits_ready
            logits_copied logits_shifted route_exp route_step weights_routed zero_column content_ready
            position_ready position_copied scores_ready exps_ready probs_turned probs_lo probs_times_v
            sums_inverted heads_normed gate_ready linear_ready tanh_ready silu_ready hidden_ready hidden_hi
            hidden_lo down_ready expert_added waits_met tile_gathered last_turned last_copied last_projected
            last_added""".split()
        s = {n: sem(n) for n in names}
        s_bdw = [sem(f"bd_written{g}") for g in range(GH)]
        s_rec = [sem("records_written0"), sem("records_written1")]
        s_slot = [sem(f"slot{g}_loaded") for g in range(GH)]
        s_bdr = [sem(f"bd_read{g}") for g in range(GH)]
        s_out = sem("out_written")
        s_w = [s["weights_loaded0"], s["weights_loaded1"]]

        block = ctx.enter_context(nc.Block())

        def ge(eng, name, value):
            if isinstance(value, int) and value < 1:
                return
            eng.wait_ge(s[name] if isinstance(name, str) else name, value)

        def met(eng):
            eng.sem_inc(s["waits_met"], 1)

        def hi_lo_terms(n):
            return [(0, 0), (0, 1), (1, 0), (1, 1)][:n]

        def write_scores(eng, n, g):
            ge(eng, "position_copied", U * n + T * (g + 1))
            if not isinstance(n, int):
                met(eng)
            if not isinstance(n, int) or n > 0:
                ge(eng, s_bdr[g], 16 * n)
                met(eng)
            eng.dma_start(scratch[g].rearrange("(p w) -> p w", p=P),
                          bdw[:, g, :, :].rearrange("p t s -> p (t s)")).then_inc(s_bdw[g], 16)

        @block.sync
        def _(sp):
            def load_x(b0, b1):
                sp.dma_start(acc[:, b0:b1, :, :].rearrange("p b t d -> p b (t d)"),
                             x[b0:b1].rearrange("b (p t) d -> p b (t d)", t=T)).then_inc(s["x_loaded"], 16)

            load_x(0, 1)
            for r, a in enumerate((bq, bk, u, v, gamma, beta)):
                a1 = a.rearrange("h d -> (h d)") if len(a.shape) == 2 else a
                sp.dma_start(rows[r:r + 1, :], a1.rearrange("(a d) -> a d", a=1)).then_inc(s["rows_loaded"], 16)
            for dst, a in ((wp_sb, Wpos), (pe_sb, peT), (idf[:, :], ident)):
                sp.dma_start(dst, a).then_inc(s["rows_loaded"], 16)
            for dst, a in ((selb[:, :, :, :], sel), (wr_f, Wr), (wq_sb, Wq), (wk_sb, Wk), (wv_sb, Wv), (wf_sb[:, :], Wf)):
                sp.dma_start(dst, a).then_inc(s["consts_loaded"], 16)
            sp.dma_start(bv_bc, bv.partition_broadcast(P)).then_inc(s["consts_loaded"], 16)
            sp.dma_start(bf_bc, bf.partition_broadcast(P)).then_inc(s["consts_loaded"], 16)
            sp.dma_start(order_bc, order.partition_broadcast(P)).then_inc(s["order_loaded"], 16)
            sp.wait_ge(s["x_loaded"], 16)
            load_x(1, B)
            def load_expert(e, r):
                ge(sp, "w2_lo", e - 1)
                if not isinstance(e, int):
                    met(sp)
                sp.dma_start(wstage[:, r, :], W13[e] if isinstance(e, int) else
                             W13[ds(e, 1)].rearrange("a p f -> p (a f)")).then_inc(s_w[r], 16)
                w2_e = W2[ds(e, 1)].rearrange("a f d -> (a f) d")
                sp.dma_start(w2stage[:, r, 0:FT - 1, :],
                             w2_e[0:(FT - 1) * P, :].rearrange("(f p) d -> p f d", p=P)).then_inc(s_w[r], 16)
                sp.dma_start(w2stage[0:FW[-1], r, FT - 1, :], w2_e[(FT - 1) * P:F, :]).then_inc(s_w[r], 16)

            def write_records(b, r):
                for name, j, src, ahead, parts in (("qv_lo", 0, quT, GH, (0, 0, 1, 1)), ("qv_lo", 2, qvT, 0, (0, 0, 1, 1)),
                                                   ("k_lo", 1, kT, GH, (0, 1, 0, 1))):
                    ge(sp, name, b + 1)
                    if not isinstance(b, int):
                        met(sp)
                    for c, part in enumerate(parts):
                        sp.dma_start(records[ds(b * H + ahead, H), HD * c:HD * (c + 1), j, :],
                                     src[:, part, r, :]).then_inc(s_rec[r], 16)

            def load_slot(n, g):
                if not isinstance(n, int) or n >= 0:
                    ge(sp, "position_ready", U * n + T * (g + 1))
                    met(sp)
                    if not isinstance(n, int) or n > 0:
                        ge(sp, "content_ready", U * (n - 1) + T * (g + 1))
                        met(sp)
                rows_g = slice(SLOT * g, SLOT * (g + 1))
                known = isinstance(n, int)
                j0, j1 = 2 if known and n < 0 else 0, 2 if known and n == N - 1 else 3
                sp.dma_start(slots[rows_g, j0:j1, :],
                             records[ds((n + 1) * GH + g, 1), :, j0:j1, :].rearrange("a r j s -> (a r) j s")
                             ).then_inc(s_slot[g], 16)
                if j1 == 3:
                    m = (n + 1) % NG
                    sp.dma_start(ps[rows_g, :], pall[rows_g, ds(m, 1), :].rearrange("p a s -> p (a s)")
                                 ).then_inc(s_slot[g], 16)

            for r in range(2):
                load_expert(r, r)
            for r in range(2):
                write_records(r, r)
                load_expert(2 + r, r)
            sp.wait_ge(s["pos_slots_copied"], NG)
            sp.wait_ge(s_rec[0], 16 * 12)
            for g in range(GH):
                load_slot(-1, g)
            with sp.Fori(1, B // 2 - 1) as i:
                for r in range(2):
                    write_records(2 * i + r, r)
                    load_expert(2 * i + 2 + r, r)
            def read_scores(n, g):
                ge(sp, s_bdw[g], 16 * (n + 1))
                met(sp)
                ge(sp, "probs_turned", U * (n - 1) + T * (g + 1))
                met(sp)
                sp.dma_start(bdr[:, g, :, :].rearrange("p t s -> p (t s)"),
                             scratch[g, S:S * (S + 1)].rearrange("(p w) -> p w", p=P)).then_inc(s_bdr[g], 16)

            write_records(B - 2, 0)
            for g in range(2):
                load_slot(0, g)
                read_scores(0, g)
            for g in range(2, GH):
                load_slot(0, g)
            ge(sp, "qkv_ready", 3 * B)
            read_scores(0, 2)
            write_records(B - 1, 1)
            for r in range(2):
                ge(sp, s_rec[r], 16 * 12 * B // 2)

            def body(n, last):
                for g in range(GH):
                    if not last:
                        load_slot(n + 1, g)
                    if g + RA < GH:
                        read_scores(n, g + RA)
                    elif not last:
                        read_scores(n + 1, g + RA - GH)
                    if not last:
                        write_scores(sp, n + 1, g)

            body(0, False)
            with sp.Fori(1, N - 2) as n:
                body(n, False)
            body(N - 2, False)
            body(N - 1, True)

            for b in range(B):
                ge(sp, "expert_added", T * (NU * NG * (E - 1) + b + 1))
                ge(sp, "tile_added", NG * (b + 1)) if b < B - 1 else ge(sp, "last_added", 1)
                sp.dma_start(out[b].rearrange("(p t) d -> p (t d)", t=T),
                             acc[:, b, :, :].rearrange("p t d -> p (t d)")).then_inc(s_out, 16)
            sp.wait_ge(s_out, 16 * B)

        @block.gpsimd
        def _(pool):
            pool.memset(bdw[:, :, :, 0:1], 0.0).then_inc(s["zero_column"], 1)
            for e in range(E):
                r = e % 2
                pool.wait_ge(s_w[r], 48 * (e // 2 + 1))
                pool.tensor_copy(w13[:, 0, e, :], wstage[:, r, :]).then_inc(s["w13_hi"], 1)
                pool.tensor_copy(w2[:, 0, e, 0:FT - 1, :], w2stage[:, r, 0:FT - 1, :]).then_inc(s["w2_hi"], 1)
                pool.tensor_copy(w2[0:FW[-1], 0, e, FT - 1, :], w2stage[0:FW[-1], r, FT - 1, :]).then_inc(s["w2_hi"], 1)
                pool.wait_ge(s["w13_hi"], e + 1)
                pool.tensor_tensor(w13[:, 1, e, :], wstage[:, r, :], w13[:, 0, e, :], ALU.subtract).then_inc(s["w13_lo"], 1)
                pool.wait_ge(s["w2_hi"], 2 * e + 2)
                pool.tensor_tensor(w2[:, 1, e, 0:FT - 1, :], w2stage[:, r, 0:FT - 1, :], w2[:, 0, e, 0:FT - 1, :],
                                   ALU.subtract)
                pool.wait_ge(s["w13_lo"], e + 1)
                pool.tensor_tensor(w2[0:FW[-1], 1, e, FT - 1, :], w2stage[0:FW[-1], r, FT - 1, :],
                                   w2[0:FW[-1], 0, e, FT - 1, :], ALU.subtract).then_inc(s["w2_lo"], 1)
            pool.wait_ge(s["consts_loaded"], 16 * 8)
            for b in range(B):
                pool.wait_ge(s["normed1"], b + 1)
                pool.tensor_tensor(acc[:, b, :, :], acc[:, b, :, :],
                                   bf_bc.unsqueeze(1).broadcast_to([P, T, D]), ALU.add).then_inc(s["bias_added"], 1)

            def split_hidden(n, su, f):
                j = NU * FT * n + FT * su + f
                w = FW[f]
                ge(pool, "hidden_ready", j + 1)
                ge(pool, "down_ready", T * (NU * (n - 1) + su + 1))
                met(pool)
                pool.tensor_copy(hh[0:w, su, f, :], hb[0:w, j_ring(su, f), :]).then_inc(s["hidden_hi"], 1)
                ge(pool, "hidden_hi", j + 1)
                pool.tensor_tensor(hl[0:w, su, f, :], hb[0:w, j_ring(su, f), :], hh[0:w, su, f, :], ALU.subtract).then_inc(s["hidden_lo"], 1)

            def norm_heads(n):
                ge(pool, "outs_copied", n + 1)
                o = ob[:, :].rearrange("p (i k d) -> p i k d", k=2, d=HD)
                pool.tensor_tensor(tmp[:, :, :], o[:, :, 0, :], o[:, :, 1, :], ALU.add).then_inc(s["outs_summed"], 1)
                ge(pool, "outs_summed", n + 1)
                ge(pool, "sums_inverted", n + 1)
                out_n = heads[:, ds(n, 1), :].rearrange("p a m -> p (a m)").rearrange("p (i d) -> p i d", d=HD)
                pool.tensor_tensor(out_n, tmp[:, :, :], rs[:, :].unsqueeze(2).broadcast_to([P, U, HD]),
                                   ALU.mult).then_inc(s["heads_normed"], 1)

            def gather_tile(n):
                b, t = n // NG - 1, n % NG
                ge(pool, "heads_normed", n // NG * NG)
                ge(pool, "tile_projected", n - NG)
                if not isinstance(n, int):
                    met(pool)
                src = heads[:, ds(b * NG, NG), :].rearrange("p m (g t d) -> p (m g) t d", g=GH, t=T)
                pool.tensor_copy(turned[:, :].rearrange("p (h a d) -> p h a d", a=1, d=HD),
                                 src[:, :, ds(t, 1), :]).then_inc(s["tile_gathered"], 1)

            def body(n, first=False, project=False):
                for i in range(U):
                    if i == LV and not first:
                        norm_heads(n - 1)
                    if i == GATHER_AT and project:
                        gather_tile(n)
                    if i in LINEAR_AT:
                        split_hidden(n, *LINEAR_AT[i])

            body(0, first=True)
            with pool.Fori(1, NG) as n:
                body(n)
            body(NG, project=True)
            with pool.Fori(NG + 1, N) as n:
                body(n, project=True)
            norm_heads(N - 1)
            pool.wait_ge(s["heads_normed"], N)
            src = heads[:, (B - 1) * NG:B * NG, :].rearrange("p m (g t d) -> p (m g) t d", g=GH, t=T)
            for t in range(T):
                ins = pool.tensor_copy(last[:, t, :].rearrange("p (h d) -> p h d", d=HD), src[:, :, t, :])
            ins.then_inc(s["tile_gathered"], 1)

        @block.scalar
        def _(act):
            act.wait_ge(s["variance1"], 1)
            act.activation(sd1, sd1, ACT.Sqrt).then_inc(s["root1"], 1)
            act.wait_ge(s["variance2"], 1)
            act.activation(sd2, sd2, ACT.Sqrt).then_inc(s["root2"], 1)
            act.wait_ge(s["rows_turned"], 1)
            act.activation(cols[:, 0:6], misc[:, 0:6], ACT.Copy).then_inc(s["cols_copied"], 1)
            act.wait_ge(s["pos_keys_ready"], 1)
            act.activation(pT_h, bank[2][:, :], ACT.Copy).then_inc(s["pos_keys_hi"], 1)
            for g in range(NG):
                act.wait_ge(s["pos_slots_ready"], g + 1)
                act.activation(pall[:, g, :], bank[3 + g % 2][:, :], ACT.Copy).then_inc(s["pos_slots_copied"], 1)
            act.wait_ge(s["cols_summed"], 2)
            def of_batch(a, b):
                return a[:, 0, ds(b, 1), :].rearrange("p a s -> p (a s)")

            def high_q(b, r):
                if isinstance(b, int):
                    ge(act, s_rec[r], 16 * 12 * (b // 2))
                else:
                    ge(act, s_rec[r], 8 * 12 * (b - r))
                ge(act, "qkv_ready", 3 * b + 1)
                act.activation(quT[:, 0, r, :], bank[3][:, :], ACT.Identity, bias=cols[:, 6:7]).then_inc(s["qu_hi"], 1)
                act.activation(qvT[:, 0, r, :], bank[3][:, :], ACT.Identity, bias=cols[:, 7:8]).then_inc(s["qv_hi"], 1)

            def high_k(b, r):
                ge(act, "qkv_ready", 3 * b + 2)
                act.activation(kT[:, 0, r, :], bank[4][:, :], ACT.Identity, bias=cols[:, 1:2]).then_inc(s["k_hi"], 1)

            def high_v(b):
                ge(act, "v_ready", b + 1)
                for c in range(T):
                    ins = act.activation(v_part(b, c, 0), v_rows(c), ACT.Copy)
                ins.then_inc(s["v_hi"], 1)

            def evac_scores(n, i):
                g, t = divmod(i, T)
                if t == 0:
                    ge(act, s_bdw[g], 16 * n)
                ge(act, "position_ready", U * n + i + 1)
                src = x3_ps if isinstance(n, int) and n == 0 and i % 2 else bd_ps
                act.activation(bdw[:, g, t, 1:S + 1], src[:, :], ACT.Copy).then_inc(s["position_copied"], 1)

            def batch(b, r, first=False):
                if not first:
                    ge(act, "variance1", b + 1)
                    act.activation(sd1, sd1, ACT.Sqrt).then_inc(s["root1"], 1)
                    high_q(b - 1, 1 - r)
                    ge(act, "variance2", b + 1)
                    act.activation(sd2, sd2, ACT.Sqrt).then_inc(s["root2"], 1)
                    high_k(b - 1, 1 - r)
                ge(act, "normed1_turned", b + 1)
                act.activation(of_batch(xnT, b), bank[0][:, :], ACT.Copy).then_inc(s["x_hi"], 1)
                ge(act, "normed2_turned", b + 1)
                act.activation(x2T[:, r, :].rearrange("p (q t) -> p q t", t=T),
                               bank[1][:, :].rearrange("p (t q) -> p q t", t=T),
                               ACT.Identity, bias=cols[:, 5:6], scale=cols[:, 4:5]).then_inc(s["x2T_ready"], 1)
                if not first:
                    high_v(b - 1)

            batch(0, 0, first=True)
            batch(1, 1)
            with act.Fori(1, B // 2) as i:
                for r in range(2):
                    batch(2 * i + r, r)
            high_q(B - 1, 1)
            high_k(B - 1, 1)
            high_v(B - 1)

            def softmax_exp(n, i):
                k = U * n + i
                ge(act, "scores_ready", k + 1)
                e = bdr[:, i // T, i % T, :]
                act.activation(e, e, ACT.Exp, bias=nmax[:, i:i + 1], scale=-1.0,
                               accum_out=sums[:, ds(n % 2, 1), i:i + 1].rearrange("p a b -> p (a b)")).then_inc(s["exps_ready"], 1)

            def evac_hi(n, i):
                k = U * n + i
                ge(act, "probs_turned", k + 1)
                ge(act, "probs_times_v", k - 1)
                act.activation(PTh[:, i % 2, :], tp_ps[i % 2][:, :], ACT.Copy).then_inc(s["probs_hi"], 1)

            def gate(n, su, f):
                j = NU * FT * n + FT * su + f
                w = FW[f]
                ge(act, "gate_ready", j + 1)
                ge(act, "hidden_lo", j - 1)
                act.activation(hb[0:w, j_ring(su, f), :], x1_ps[0:w, :], ACT.Tanh, scale=0.5).then_inc(s["tanh_ready"], 1)

            def body(n, first, last, project=False):
                for i in range(U):
                    if not last:
                        evac_scores(n + 1, i)
                    if i - 1 in GATE_AT:
                        gate(n, *GATE_AT[i - 1])
                    softmax_exp(n, i)
                    if i >= LT:
                        evac_hi(n, i - LT)
                    elif not first:
                        evac_hi(n - 1, U + i - LT)
                    if i == TURN_AT and project:
                        evac_turned(n)

            def evac_turned(n):
                ge(act, "tile_turned", n - NG + 1)
                act.activation(turned[:, :], y_ps[:, 0:P], ACT.Copy).then_inc(s["turned_copied"], 1)

            act.wait_ge(s["zero_column"], 1)
            for i in range(U):
                if i == 2:
                    act.wait_ge(s["logits_shifted"], 1)
                    act.activation(lg, lg, ACT.Exp).then_inc(s["route_exp"], 1)
                evac_scores(0, i)
                if i % T == T - 1:
                    write_scores(act, 0, i // T)
            body(0, True, False)
            with act.Fori(1, NG) as n:
                body(n, False, False)
            with act.Fori(NG, N - 2) as n:
                body(n, False, False, project=True)
            body(N - 2, False, False, project=True)
            body(N - 1, False, True, project=True)
            for i in range(U - LT, U):
                evac_hi(N - 1, i)
            ge(act, "last_turned", 1)
            act.activation(lastT, bank[0][:, :], ACT.Copy).then_inc(s["last_copied"], 1)

        @block.tensor
        def _(pe):
            pe.wait_ge(s["rows_loaded"], 16 * 9)
            pe.transpose(misc[:, 0:6], rows, idf[0:6, 0:6]).then_inc(s["rows_turned"], 1)
            pe.matmul(bank[2][:, :], wp_sb, pe_sb, start=True, stop=True).then_inc(s["pos_keys_ready"], 1)
            pe.wait_ge(s["consts_loaded"], 16 * 8)
            pe.wait_ge(s["pos_keys_hi"], 1)
            pe.wait_ge(s["pos_keys_lo"], 1)
            for g in range(NG):
                ge(pe, "pos_slots_copied", g - 1)
                for part, src in enumerate((pT_h, pT_l)):
                    mm = pe.matmul(bank[3 + g % 2][:, :], selb[:, part, g, :], src, start=(part == 0), stop=(part == 1))
                mm.then_inc(s["pos_slots_ready"], 1)
            pe.wait_ge(s["pos_slots_copied"], NG)
            pe.wait_ge(s["wr_lo"], 1)
            def position_scores(n, i):
                g, t = divmod(i, T)
                if t == 0:
                    ge(pe, s_slot[g], 32 * (n + 1))
                dst = bd_ps
                if isinstance(n, int) and n == 0:
                    dst = x3_ps if i % 2 else bd_ps
                    ge(pe, "position_copied", i - 1)
                else:
                    ge(pe, "position_copied", U * n + i)
                r = slice(SLOT * g, SLOT * (g + 1))
                pe.matmul(dst[:, :], qvs[r, t * P:(t + 1) * P], ps[r, :], start=True, stop=True).then_inc(s["position_ready"], 1)

            def batch(b, r):
                pe.wait_ge(s["normed1"], b + 1)
                ge(pe, "x_lo", b)
                for t in range(T):
                    mm = pe.transpose(bank[0][:, t * P:(t + 1) * P], xn1[:, r, t, :],
                                      idf[:, :])
                mm.then_inc(s["normed1_turned"], 1)
                pe.wait_ge(s["normed2"], b + 1)
                ge(pe, "x2T_ready", b)
                for t in range(T):
                    mm = pe.transpose(bank[1][:, t * P:(t + 1) * P], xn2[:, r, t, :],
                                      idf[:, :])
                mm.then_inc(s["normed2_turned"], 1)
                pe.wait_ge(s["x2T_ready"], b + 1)
                xt = x2T[:, r, :]
                ge(pe, "qv_lo", b)
                pe.matmul(bank[3][:, :].rearrange("p (t q) -> p t q", t=T), wq_sb,
                          xt.rearrange("p (q t) -> p t q", t=T), start=True, stop=True).then_inc(s["qkv_ready"], 1)
                ge(pe, "k_lo", b)
                pe.matmul(bank[4][:, :], wk_sb, xt, start=True, stop=True).then_inc(s["qkv_ready"], 1)
                ge(pe, "v_ready", b)
                for c in range(T):
                    mm = pe.matmul(bank[5][:, c * D:(c + 1) * D],
                                   x2T[:, r, c * P:(c + 1) * P], wv_sb, start=True, stop=True)
                mm.then_inc(s["qkv_ready"], 1)
                pe.wait_ge(s["x_lo"], b + 1)
                terms = hi_lo_terms(4)
                for t in range(T):
                    for m, (a, w) in enumerate(terms):
                        mm = pe.matmul(misc[:, ds((b * T + t) * E, E)],
                                       xnT[:, a, ds(b, 1), t * P:(t + 1) * P].rearrange("p a s -> p (a s)"),
                                       wr_l if w else wr_h, start=(m == 0), stop=(m == 3))
                mm.then_inc(s["logits_ready"], 1)

            batch(0, 0)
            batch(1, 1)
            with pe.Fori(1, B // 2) as i:
                for r in range(2):
                    batch(2 * i + r, r)
            for i in range(U):
                position_scores(0, i)
            def content_scores(n, i):
                g, t = divmod(i, T)
                if t == 0:
                    ge(pe, s_slot[g], 32 * N + 16 if isinstance(n, int) and n == N - 1 else 32 * (n + 2))
                ge(pe, "scores_ready", U * n + i)
                r = slice(SLOT * g, SLOT * (g + 1))
                pe.matmul(ac_ps[:, :], qus[r, t * P:(t + 1) * P], ks[r, :], start=True, stop=True).then_inc(s["content_ready"], 1)

            def transposes(n, i):
                k = U * n + i
                ge(pe, "exps_ready", k + 1)
                ge(pe, "probs_lo", k - 1)
                for c in range(T):
                    mm = pe.transpose(tp_ps[i % 2][:, c * P:(c + 1) * P], bdr[:, i // T, i % T, c * P:(c + 1) * P], idf[:, :])
                mm.then_inc(s["probs_turned"], 1)

            def weighted_v(n, i):
                g, t = divmod(i, T)
                k = U * n + i
                ge(pe, "probs_lo", k + 1)
                if i == 0:
                    ge(pe, "outs_copied", n)
                steps = [(c, pt) for c in range(T) for pt in (PTh, PTl)]
                for m, (c, pt) in enumerate(steps):
                    mm = pe.matmul(misc[:, i * 2 * HD:(i + 1) * 2 * HD], pt[:, i % 2, c * P:(c + 1) * P],
                                   vv[:, ds(n, 1), c, g, :, :].rearrange("p a k d -> p (a k d)"),
                                   start=(m == 0), stop=(m == len(steps) - 1))
                mm.then_inc(s["probs_times_v"], 1)

            def hidden(n, su, f, linear):
                j = NU * FT * n + FT * su + f
                w = FW[f]
                dst, o, free, done = (x3_ps, F, "hidden_ready", "linear_ready") if linear else (x1_ps, 0, "silu_ready", "gate_ready")
                ge(pe, free, j)
                e, b = n // NG, NU * (n % NG) + su
                for m, (wp, xp) in enumerate(hi_lo_terms(3)):
                    mm = pe.matmul(dst[0:w, :],
                                   w13[:, wp, ds(e, 1), o + P * f:o + P * f + w].rearrange("p a m -> p (a m)"),
                                   xnT[:, xp, ds(b, 1), :].rearrange("p a s -> p (a s)"),
                                   start=(m == 0), stop=(m == 2))
                mm.then_inc(s[done], 1)

            def down(n, su, t):
                y = T * (NU * n + su) + t
                e = n // NG
                if t == 0:
                    ge(pe, "hidden_lo", FT * (NU * n + su) + FT)
                    ge(pe, "expert_added", T * (NU * n + su))
                o = t * D
                steps = [(f, hp, wp) for f in range(FT) for hp, wp in hi_lo_terms(3)]
                for m, (f, hp, wp) in enumerate(steps):
                    w = FW[f]
                    h = (hl if hp else hh)[0:w, su, f, t * P:(t + 1) * P]
                    mm = pe.matmul(y_ps[:, o:o + D], h, w2[0:w, wp, ds(e, 1), f, :].rearrange("p a d -> p (a d)"),
                                   start=(m == 0), stop=(m == len(steps) - 1))
                mm.then_inc(s["down_ready"], 1)

            def turn_tile(n):
                ge(pe, "tile_gathered", n - NG + 1)
                ge(pe, "expert_added", T * NU * n)
                pe.transpose(y_ps[:, 0:P], turned[:, :], idf[:, :]).then_inc(s["tile_turned"], 1)

            def project_tile(n):
                ge(pe, "turned_copied", n - NG + 1)
                pe.matmul(y_ps[:, 0:D], turned[:, :], wf_sb[:, :], start=True, stop=True).then_inc(s["tile_projected"], 1)

            def body(n, first, last, project=False):
                for i in range(U):
                    content_scores(n, i)
                    if not last:
                        position_scores(n + 1, i)
                    if i >= LV:
                        weighted_v(n, i - LV)
                    elif not first:
                        weighted_v(n - 1, U + i - LV)
                    if i >= LT:
                        transposes(n, i - LT)
                    elif not first:
                        transposes(n - 1, U + i - LT)
                    if project and i == TURN_AT:
                        turn_tile(n)
                    if project and i == PROJECT_AT:
                        project_tile(n)
                    if project and i == min(k for k in DOWN_AT if k > PROJECT_AT):
                        ge(pe, "tile_added", n - NG + 1)
                    if i in GATE_AT:
                        hidden(n, *GATE_AT[i], linear=False)
                    if i in LINEAR_AT:
                        hidden(n, *LINEAR_AT[i], linear=True)
                    su, tiles = DOWN_AT.get(i, (0, ()))
                    for t in tiles:
                        if not (su and first):
                            down(n - su, su, t)

            ge(pe, "position_copied", U)
            pe.wait_ge(s["logits_copied"], 1)
            pe.wait_ge(s["v_lo"], B)
            pe.wait_ge(s["k_lo"], B)
            pe.wait_ge(s["w2_lo"], E)
            body(0, True, False)
            with pe.Fori(1, NG) as n:
                body(n, False, False)
            with pe.Fori(NG, N - 2) as n:
                body(n, False, False, project=True)
            body(N - 2, False, False, project=True)
            body(N - 1, False, True, project=True)
            for i in range(U, U + LV):
                weighted_v(N - 1, i - LV)
                if i - LT < U:
                    transposes(N - 1, i - LT)

            for t in range(T):
                down(N - 1, 1, t)

            pe.wait_ge(s["tile_gathered"], N - NG + 1)
            for t in range(T):
                mm = pe.transpose(bank[0][:, t * P:(t + 1) * P], last[:, t, :], idf[:, :])
            mm.then_inc(s["last_turned"], 1)
            pe.wait_ge(s["last_copied"], 1)
            for t in range(T):
                mm = pe.matmul(bank[2][:, t * D:(t + 1) * D], lastT[:, t * P:(t + 1) * P], wf_sb[:, :],
                               start=True, stop=True)
            mm.then_inc(s["last_projected"], 1)

        @block.vector
        def _(dve):
            V = nc.vector
            def row_stats(b, src, mv, sd, s_st, s_ag, s_ve, s_nrm):
                ge(dve, s_nrm, b)
                for t in range(T):
                    V.bn_stats(st6[:, t, :], src(t)).then_inc(s[s_st], 1)
                ge(dve, s_st, T * (b + 1))
                met(dve)
                for t in range(T):
                    V.bn_aggr(mv[:, t, :], st6[:, t, :]).then_inc(s[s_ag], 1)
                ge(dve, s_ag, T * (b + 1))
                V.tensor_scalar(sd, mv[:, :, 1], EPS, None, ALU.add).then_inc(s[s_ve], 1)

            def normed(b, src, dst, mv, sd, rd, s_sd, s_rd, s_nrm):
                ge(dve, s_sd, b + 1)
                V.reciprocal(rd, sd).then_inc(s[s_rd], 1)
                ge(dve, s_rd, b + 1)
                for t in range(T):
                    ins = V.tensor_scalar(dst(t), src(t), mv[:, t, 0:1], rd[:, t:t + 1], ALU.subtract, ALU.mult)
                ins.then_inc(s[s_nrm], 1)

            def low(b, name, dst, src, hi, bias, after):
                ge(dve, after, b + 1)
                if bias is None:
                    V.tensor_tensor(dst, src, hi, ALU.subtract).then_inc(s[name], 1)
                else:
                    V.scalar_tensor_tensor(out=dst, in0=src, scalar=bias, in1=hi, op0=ALU.add,
                                           op1=ALU.subtract).then_inc(s[name], 1)

            def low_x(b):
                x_lo, x_hi = (xnT[:, k, ds(b, 1), :].rearrange("p a s -> p (a s)") for k in (1, 0))
                low(b, "x_lo", x_lo, bank[0][:, :], x_hi, None, "x_hi")

            def low_q(b, r):
                low(b, "qu_lo", quT[:, 1, r, :], bank[3][:, :], quT[:, 0, r, :], cols[:, 6:7], "qv_hi")
                low(b, "qv_lo", qvT[:, 1, r, :], bank[3][:, :], qvT[:, 0, r, :], cols[:, 7:8], "qv_hi")

            def low_k_v(b, r):
                low(b, "k_lo", kT[:, 1, r, :], bank[4][:, :], kT[:, 0, r, :], cols[:, 1:2], "k_hi")
                ge(dve, "qkv_ready", 3 * b + 3)
                ge(dve, "v_lo", b)
                V.tensor_tensor(hb[:, 0, :].rearrange("p (c d) -> p c d", c=T),
                                bank[5][:, :].rearrange("p (c d) -> p c d", c=T),
                                bv_bc.unsqueeze(1).broadcast_to([P, T, D]), ALU.add).then_inc(s["v_ready"], 1)

            def low_v(b):
                ge(dve, "v_hi", b + 1)
                for c in range(T):
                    ins = V.tensor_tensor(v_part(b, c, 1), v_rows(c), v_part(b, c, 0), ALU.subtract)
                ins.then_inc(s["v_lo"], 1)

            def norms(b, r, between=lambda: None, between2=lambda: None):
                x0 = (lambda t: acc[:, b, t, :]) if isinstance(b, int) else \
                    (lambda t: acc[:, ds(b, 1), t, :].rearrange("p a d -> p (a d)"))
                x1, x2 = (lambda t: xn1[:, r, t, :]), (lambda t: xn2[:, r, t, :])
                row_stats(b, x0, mv1, sd1, "stats1", "moments1", "variance1", "normed1")
                between()
                normed(b, x0, x1, mv1, sd1, rd1, "root1", "inverse_root1", "normed1")
                ge(dve, "normed1", b + 1)
                row_stats(b, x1, mv2, sd2, "stats2", "moments2", "variance2", "normed2")
                between2()
                normed(b, x1, x2, mv2, sd2, rd2, "root2", "inverse_root2", "normed2")

            def batch(b, r, second=False):
                norms(b, r, between=lambda: None if second else low_v(b - 2), between2=lambda: low_q(b - 1, 1 - r))
                low_x(b)
                low_k_v(b - 1, 1 - r)

            dve.wait_ge(s["x_loaded"], 16)
            norms(0, 0)
            dve.wait_ge(s["cols_copied"], 1)
            V.tensor_tensor(cols[:, 6:7], cols[:, 0:1], cols[:, 2:3], ALU.add).then_inc(s["cols_summed"], 1)
            V.tensor_tensor(cols[:, 7:8], cols[:, 0:1], cols[:, 3:4], ALU.add).then_inc(s["cols_summed"], 1)
            dve.wait_ge(s["consts_loaded"], 16 * 8)
            V.tensor_copy(wr_h, wr_f).then_inc(s["wr_hi"], 1)
            dve.wait_ge(s["wr_hi"], 1)
            V.tensor_tensor(wr_l, wr_f, wr_h, ALU.subtract).then_inc(s["wr_lo"], 1)
            dve.wait_ge(s["pos_keys_hi"], 1)
            V.tensor_tensor(pT_l, bank[2][:, :], pT_h, ALU.subtract).then_inc(s["pos_keys_lo"], 1)
            dve.wait_ge(s["cols_summed"], 2)
            low_x(0)
            dve.wait_ge(s["x_loaded"], 32)
            batch(1, 1, second=True)
            with dve.Fori(1, B // 2) as i:
                for r in range(2):
                    batch(2 * i + r, r)
            low_v(B - 2)
            low_q(B - 1, 1)
            low_k_v(B - 1, 1)
            low_v(B - 1)

            chain = [0]

            def step(ins):
                ins.then_inc(s["route_step"], 1)
                chain[0] += 1
                dve.wait_ge(s["route_step"], chain[0])

            dve.wait_ge(s["logits_ready"], B)
            dve.wait_ge(s["order_loaded"], 16)
            dve.wait_ge(s["w2_lo"], E)
            V.tensor_copy(lg, misc[:, 0:BT * E].rearrange("p (i e) -> p i e", e=E)).then_inc(s["logits_copied"], 1)
            dve.wait_ge(s["logits_copied"], 1)
            step(V.tensor_reduce(mx, lg, AX.X, ALU.max))
            V.tensor_tensor(lg, lg, mx.unsqueeze(2).broadcast_to([P, BT, E]), ALU.subtract).then_inc(s["logits_shifted"], 1)
            dve.wait_ge(s["route_exp"], 1)
            order = order_bc.unsqueeze(1).broadcast_to([P, BT, E])
            spread = lambda a: a.unsqueeze(2).broadcast_to([P, BT, E])
            left = lg
            for k in range(TOPK):
                step(V.tensor_reduce(mx, left, AX.X, ALU.max))
                step(V.tensor_tensor(at[k], left, spread(mx), ALU.is_equal))
                step(V.tensor_tensor(at[k], at[k], order, ALU.mult))
                step(V.tensor_reduce(mx, at[k], AX.X, ALU.max))
                step(V.tensor_tensor(at[k], order, spread(mx), ALU.is_equal))
                if k == 0:
                    left = rest
                    step(V.scalar_tensor_tensor(out=rest, in0=at[0], scalar=-2.0, in1=lg, op0=ALU.mult, op1=ALU.add))
            step(V.tensor_tensor(at[0], at[0], at[1], ALU.add))
            step(V.scalar_tensor_tensor(out=rank, in0=at[0], scalar=0.5, in1=lg, op0=ALU.mult, op1=ALU.mult))
            step(V.tensor_reduce(den, rank, AX.X, ALU.add))
            step(V.tensor_scalar(den, den, 2.0, None, ALU.mult))
            step(V.reciprocal(rden, den))
            V.tensor_tensor(cw[:, :, :], rank, rden.unsqueeze(2).broadcast_to([P, BT, E]), ALU.mult).then_inc(s["weights_routed"], 1)
            dve.wait_ge(s["bias_added"], B)
            dve.wait_ge(s["weights_routed"], 1)

            def add_scores(n, i):
                g, t = divmod(i, T)
                k = U * n + i
                ge(dve, "content_ready", k + 1)
                if t == 0:
                    ge(dve, s_bdr[g], 16 * (n + 1))
                ge(dve, "exps_ready", k - U + 1) if not isinstance(n, int) or n > 0 else None
                met(dve)
                V.tensor_tensor_reduce(out=bdr[:, g, t, :], in0=ac_ps[:, :], in1=bdr[:, g, t, :],
                                       scale=-SCALE, scalar=3.0e38, op0=ALU.add, op1=ALU.min,
                                       accum_out=nmax[:, i:i + 1]).then_inc(s["scores_ready"], 1)

            def evac_T(n, i):
                k = U * n + i
                ge(dve, "probs_hi", k + 1)
                ge(dve, "probs_times_v", k - 1)
                V.tensor_tensor(PTl[:, i % 2, :], tp_ps[i % 2][:, :], PTh[:, i % 2, :], ALU.subtract).then_inc(s["probs_lo"], 1)

            def evac_out(n):
                ge(dve, "probs_times_v", U * (n + 1))
                ge(dve, "heads_normed", n)
                V.tensor_copy(ob[:, :], misc[:, 0:U * 2 * HD]).then_inc(s["outs_copied"], 1)
                V.reciprocal(rs[:, :], sums[:, ds(n % 2, 1), :].rearrange("p a i -> p (a i)")).then_inc(s["sums_inverted"], 1)

            def silu2(n, su, f):
                j = NU * FT * n + FT * su + f
                w = FW[f]
                ge(dve, "tanh_ready", j + 1)
                h = hb[0:w, j_ring(su, f), :]
                V.scalar_tensor_tensor(out=h, in0=h, scalar=1.0, in1=x1_ps[0:w, :], op0=ALU.add,
                                       op1=ALU.mult).then_inc(s["silu_ready"], 1)

            def times_linear(n, su, f):
                j = NU * FT * n + FT * su + f
                w = FW[f]
                ge(dve, "linear_ready", j + 1)
                ge(dve, "silu_ready", j + 1)
                h = hb[0:w, j_ring(su, f), :]
                V.tensor_tensor(h, h, x3_ps[0:w, :], ALU.mult).then_inc(s["hidden_ready"], 1)

            def add_expert(n, su, t):
                y = T * (NU * n + su) + t
                e, b = n // NG, NU * (n % NG) + su
                ge(dve, "down_ready", T * (NU * n + su + 1))
                ge(dve, "expert_added", T * (NU * n + su))
                a = acc[:, ds(b, 1), t, :].rearrange("p a d -> p (a d)")
                V.scalar_tensor_tensor(out=a, in0=y_ps[:, t * D:(t + 1) * D],
                                       scalar=cw[:, ds(b * T + t, 1), ds(e, 1)].rearrange("p a e -> p (a e)"),
                                       in1=a, op0=ALU.mult, op1=ALU.add).then_inc(s["expert_added"], 1)

            def add_experts(n, i, first):
                for ago, tiles in ((1, range(0, T // 2)), (2, range(T // 2, T))):
                    su, products = DOWN_AT.get(i - ago, (0, ()))
                    if T - 1 in products and not (su and first):
                        for t in tiles:
                            add_expert(n - su, su, t)

            def add_tile(n):
                ge(dve, "tile_projected", n - NG + 1)
                ge(dve, "expert_added", T * NU * n)
                a = acc[:, ds(n // NG - 1, 1), ds(n % NG, 1), :].rearrange("p a t d -> p (a t d)")
                V.tensor_tensor(a, a, y_ps[:, 0:D], ALU.add).then_inc(s["tile_added"], 1)

            def body(n, first, last, project=False):
                for i in range(U):
                    add_scores(n, i)
                    if i >= LL:
                        evac_T(n, i - LL)
                    elif not first:
                        evac_T(n - 1, U + i - LL)
                    if i == LV - 1 and not first:
                        evac_out(n - 1)
                    if i - 1 in GATE_AT:
                        silu2(n, *GATE_AT[i - 1])
                    if i - 1 in LINEAR_AT:
                        times_linear(n, *LINEAR_AT[i - 1])
                    if i == 0 and not first:
                        times_linear(n - 1, *LINEAR_AT[U - 1])
                    if i - 1 == PROJECT_AT and project:
                        add_tile(n)
                    add_experts(n, i, first)

            body(0, True, False)
            with dve.Fori(1, NG) as n:
                body(n, False, False)
            with dve.Fori(NG, N - 2) as n:
                body(n, False, False, project=True)
            body(N - 2, False, False, project=True)
            body(N - 1, False, True, project=True)
            for i in range(U - LL, U):
                evac_T(N - 1, i)
            times_linear(N - 1, *LINEAR_AT[U - 1])
            evac_out(N - 1)
            for t in range(T):
                add_expert(N - 1, 1, t)

            dve.wait_ge(s["last_projected"], 1)
            dve.wait_ge(s["expert_added"], T * NU * N)
            a = acc[:, B - 1, :, :].rearrange("p t d -> p (t d)")
            V.tensor_tensor(a, a, bank[2][:, :], ALU.add).then_inc(s["last_added"], 1)


_INS = ['L0_attn_x', 'L0_attn_Wq', 'L0_attn_bq', 'L0_attn_Wk', 'L0_attn_bk', 'L0_attn_Wv', 'L0_attn_bv',
        'L0_attn_Wpos', 'L0_attn_Wf', 'L0_attn_bf', 'L0_attn_u', 'L0_attn_v', 'L0_attn_gamma', 'L0_attn_beta',
        'L0_ffn_W13', 'L0_ffn_W2', 'L0_ffn_Wr']


def shape_constants(S, D, H, HD, E):
    import numpy as np

    pos = np.arange(S, dtype=np.float32)
    inv_freq = (np.float32(1.0) / np.power(np.float32(10000.0), np.arange(0.0, D, 2.0, dtype=np.float32) / np.float32(D)))
    angles = pos[:, None] * inv_freq[None, :].astype(np.float32)
    pe = np.zeros((S, D), np.float32)
    pe[:, 0::2] = np.sin(angles)
    pe[:, 1::2] = np.cos(angles)
    sel = np.zeros((H, HD, 2, H // 4, 4, 4, HD), np.float16)
    for h in range(H):
        for d in range(HD):
            for copy, part in enumerate((0, 1, 0, 1)):
                sel[h, d, part, h // 4, h % 4, copy, d] = 1.0
    return {
        "peT": np.ascontiguousarray(pe.T), "ident": np.eye(128, dtype=np.float32),
        "sel": sel.reshape(H * HD, 2, H // 4, 128), "order": np.arange(E, 0, -1, dtype=np.float32),
    }


def kernel(**inputs):
    import numpy as _np
    import concourse.bacc as _bacc
    from concourse import mybir as _mybir
    from concourse.bass_utils import run_bass_kernel_spmd as _run

    nc = _bacc.Bacc("TRN2", target_bir_lowering=False, num_devices=1)
    arrays, args = {}, []
    given = {n: _np.ascontiguousarray(inputs[n]) for n in _INS}
    B, S, D = given['L0_attn_x'].shape
    H, HD = given['L0_attn_u'].shape
    E = given['L0_ffn_Wr'].shape[1]
    given.update(shape_constants(S, D, H, HD, E))
    for name, a in given.items():
        arrays[f"in_{name}_dram"] = a
        args.append(nc.dram_tensor(f"in_{name}_dram", a.shape, _mybir.dt.from_np(a.dtype), kind="ExternalInput").ap())
    args.append(nc.dram_tensor("out_0_dram", (B, S, D), F32, kind="ExternalOutput").ap())
    build(nc, *args)
    r = _run(nc, [arrays], core_ids=[0])
    return r.results[0]["out_0_dram"]
```
